# Optimizing a Trainium2 kernel written in Bass

```python
import numpy as np
import jax
import jax.numpy as jnp

def _softmax(x, axis=-1):
    return jax.nn.softmax(x, axis=axis)

def _gelu(x):
    return jax.nn.gelu(x, approximate=True)

def _silu(x):
    return jax.nn.silu(x)

def _sigmoid(x):
    return jax.nn.sigmoid(x)

def _layernorm(x, axis=-1, eps=1e-05):
    m = jnp.mean(x, axis=axis, keepdims=True)
    v = jnp.var(x, axis=axis, keepdims=True)
    return (x - m) / jnp.sqrt(v + eps)

def _scatter_add(tgt, idx, src, axis=0):
    return tgt.at[idx].add(src)

def _segment_sum(src, seg, n):
    return jax.ops.segment_sum(src, seg, n)
kernel_name = 'mk_seq_preln_d1_jaxref_r4_bfd567'

def setup_inputs(seed: int=0):
    np.random.seed(seed)
    _w = jnp.asarray

    def _L0_attn_setup():
        import jax, jax.numpy as jnp
        import numpy as np
        EMBED = 512
        D_COMPR = 128
        D_ROPE = 128
        N_HEADS = 8
        HEAD_DIM = D_COMPR // N_HEADS
        B, S = (4, 512)

        def _lin(x, w, b):
            return jnp.einsum('bsi,oi->bso', x, w) + b

        def _rope_emb(seq_len):
            inv_freq = 1.0 / 10000.0 ** (jnp.arange(0, D_ROPE, 2, dtype=jnp.float32) / D_ROPE)
            t = jnp.arange(seq_len, dtype=jnp.float32)
            freqs = jnp.einsum('i,j->ij', t, inv_freq)
            return jnp.concatenate([freqs, freqs], axis=-1)

        def _apply_rope(x, emb):
            cos, sin = (jnp.cos(emb), jnp.sin(emb))
            x1, x2 = jnp.split(x, 2, axis=-1)
            rot = jnp.concatenate([-x2, x1], axis=-1)
            return x * cos + rot * sin
        key = jax.random.key(seed)
        ks = jax.random.split(key, 20)
        sc = 0.02
        inp = {'x': jax.random.normal(ks[0], (B, S, EMBED), dtype=jnp.float32)}

        def w(k, o, i):
            return jax.random.normal(k, (o, i), dtype=jnp.float32) * sc
        inp['CQ_w'] = w(ks[1], D_COMPR, EMBED)
        inp['CQ_b'] = jnp.zeros((D_COMPR,), jnp.float32)
        inp['CQC_w'] = w(ks[2], D_COMPR - D_ROPE, D_COMPR)
        inp['CQC_b'] = jnp.zeros((D_COMPR - D_ROPE,), jnp.float32)
        inp['CQR_w'] = w(ks[3], D_ROPE, EMBED)
        inp['CQR_b'] = jnp.zeros((D_ROPE,), jnp.float32)
        inp['CKV_w'] = w(ks[4], D_COMPR, EMBED)
        inp['CKV_b'] = jnp.zeros((D_COMPR,), jnp.float32)
        inp['CKR_w'] = w(ks[5], D_ROPE, EMBED)
        inp['CKR_b'] = jnp.zeros((D_ROPE,), jnp.float32)
        inp['CKC_w'] = w(ks[6], D_COMPR - D_ROPE, D_COMPR)
        inp['CKC_b'] = jnp.zeros((D_COMPR - D_ROPE,), jnp.float32)
        inp['CV_w'] = w(ks[7], D_COMPR, D_COMPR)
        inp['CV_b'] = jnp.zeros((D_COMPR,), jnp.float32)
        inp['OUT_w'] = w(ks[8], EMBED, D_COMPR)
        inp['OUT_b'] = jnp.zeros((EMBED,), jnp.float32)
        return inp
    _L0_attn_in = _L0_attn_setup()

    def _L0_ffn_setup():
        import jax, jax.numpy as jnp
        import numpy as np
        B, S, D = (2, 512, 512)
        E, H, TOP_K = (8, 352, 2)
        SH = 352
        ROUTED_SCALE = 2.5
        key = jax.random.key(seed)
        ks = jax.random.split(key, 8)
        std = 0.02
        return {'x': jax.random.normal(ks[0], (B, S, D), jnp.float32), 'gate_w': jax.random.normal(ks[1], (E, D), jnp.float32) * std, 'w1': jax.random.normal(ks[2], (E, D, H), jnp.float32) * std, 'w3': jax.random.normal(ks[3], (E, D, H), jnp.float32) * std, 'w2': jax.random.normal(ks[4], (E, H, D), jnp.float32) * std, 'sw1': jax.random.normal(ks[5], (D, SH), jnp.float32) * std, 'sw3': jax.random.normal(ks[6], (D, SH), jnp.float32) * std, 'sw2': jax.random.normal(ks[7], (SH, D), jnp.float32) * std}
    _L0_ffn_in = _L0_ffn_setup()
    _d = {'L0_attn_x': _L0_attn_in['x'], 'L0_attn_CQ_w': _L0_attn_in['CQ_w'], 'L0_attn_CQ_b': _L0_attn_in['CQ_b'], 'L0_attn_CQC_w': _L0_attn_in['CQC_w'], 'L0_attn_CQC_b': _L0_attn_in['CQC_b'], 'L0_attn_CQR_w': _L0_attn_in['CQR_w'], 'L0_attn_CQR_b': _L0_attn_in['CQR_b'], 'L0_attn_CKV_w': _L0_attn_in['CKV_w'], 'L0_attn_CKV_b': _L0_attn_in['CKV_b'], 'L0_attn_CKR_w': _L0_attn_in['CKR_w'], 'L0_attn_CKR_b': _L0_attn_in['CKR_b'], 'L0_attn_CKC_w': _L0_attn_in['CKC_w'], 'L0_attn_CKC_b': _L0_attn_in['CKC_b'], 'L0_attn_CV_w': _L0_attn_in['CV_w'], 'L0_attn_CV_b': _L0_attn_in['CV_b'], 'L0_attn_OUT_w': _L0_attn_in['OUT_w'], 'L0_attn_OUT_b': _L0_attn_in['OUT_b'], 'L0_ffn_gate_w': _L0_ffn_in['gate_w'], 'L0_ffn_w1': _L0_ffn_in['w1'], 'L0_ffn_w2': _L0_ffn_in['w2'], 'L0_ffn_w3': _L0_ffn_in['w3'], 'L0_ffn_sw1': _L0_ffn_in['sw1'], 'L0_ffn_sw2': _L0_ffn_in['sw2'], 'L0_ffn_sw3': _L0_ffn_in['sw3']}
    _x0 = _d['L0_attn_x']
    _d['L0_attn_x'] = jax.random.normal(jax.random.fold_in(jax.random.key(seed), 1), (2, 2048, 512), dtype=_x0.dtype)
    del _x0
    return _d

def reference(L0_attn_x, L0_attn_CQ_w, L0_attn_CQ_b, L0_attn_CQC_w, L0_attn_CQC_b, L0_attn_CQR_w, L0_attn_CQR_b, L0_attn_CKV_w, L0_attn_CKV_b, L0_attn_CKR_w, L0_attn_CKR_b, L0_attn_CKC_w, L0_attn_CKC_b, L0_attn_CV_w, L0_attn_CV_b, L0_attn_OUT_w, L0_attn_OUT_b, L0_ffn_gate_w, L0_ffn_w1, L0_ffn_w2, L0_ffn_w3, L0_ffn_sw1, L0_ffn_sw2, L0_ffn_sw3):

    def _L0_attn_ref(x, CQ_w, CQ_b, CQC_w, CQC_b, CQR_w, CQR_b, CKV_w, CKV_b, CKR_w, CKR_b, CKC_w, CKC_b, CV_w, CV_b, OUT_w, OUT_b):
        import jax, jax.numpy as jnp
        import numpy as np
        EMBED = 512
        D_COMPR = 128
        D_ROPE = 128
        N_HEADS = 8
        HEAD_DIM = D_COMPR // N_HEADS
        B, S = (4, 512)

        def _lin(x, w, b):
            return jnp.einsum('bsi,oi->bso', x, w) + b

        def _rope_emb(seq_len):
            inv_freq = 1.0 / 10000.0 ** (jnp.arange(0, D_ROPE, 2, dtype=jnp.float32) / D_ROPE)
            t = jnp.arange(seq_len, dtype=jnp.float32)
            freqs = jnp.einsum('i,j->ij', t, inv_freq)
            return jnp.concatenate([freqs, freqs], axis=-1)

        def _apply_rope(x, emb):
            cos, sin = (jnp.cos(emb), jnp.sin(emb))
            x1, x2 = jnp.split(x, 2, axis=-1)
            rot = jnp.concatenate([-x2, x1], axis=-1)
            return x * cos + rot * sin
        b, s, _ = x.shape
        gelu = lambda t: jax.nn.gelu(t, approximate=False)
        cq = gelu(_lin(x, CQ_w, CQ_b))
        cqc = _lin(cq, CQC_w, CQC_b)
        cqr = _lin(x, CQR_w, CQR_b)
        ckv = gelu(_lin(x, CKV_w, CKV_b))
        ckr = _lin(x, CKR_w, CKR_b)
        ckc = _lin(ckv, CKC_w, CKC_b)
        emb = _rope_emb(s)
        cqr = _apply_rope(cqr, emb)
        ckr = _apply_rope(ckr, emb)
        Q = gelu(jnp.concatenate([cqc, cqr], axis=-1))
        K = gelu(jnp.concatenate([ckc, ckr], axis=-1))
        V = _lin(ckv, CV_w, CV_b)
        Q = Q.reshape(b, s, N_HEADS, HEAD_DIM).transpose(0, 2, 1, 3)
        K = K.reshape(b, s, N_HEADS, HEAD_DIM).transpose(0, 2, 1, 3)
        V = V.reshape(b, s, N_HEADS, HEAD_DIM).transpose(0, 2, 1, 3)
        scale = 1.0 / np.sqrt(HEAD_DIM).astype(np.float32)
        scores = jnp.einsum('bhqd,bhkd->bhqk', Q, K) * scale
        causal = jnp.triu(jnp.ones((s, s), dtype=bool), k=1)
        scores = jnp.where(causal[None, None], -jnp.inf, scores)
        attn = jax.nn.softmax(scores, axis=-1)
        out = jnp.einsum('bhqk,bhkd->bhqd', attn, V)
        out = out.transpose(0, 2, 1, 3).reshape(b, s, D_COMPR)
        return _lin(out, OUT_w, OUT_b)

    def _L0_ffn_ref(x, gate_w, w1, w2, w3, sw1, sw2, sw3):
        import jax, jax.numpy as jnp
        import numpy as np
        B, S, D = (2, 512, 512)
        E, H, TOP_K = (8, 352, 2)
        SH = 352
        ROUTED_SCALE = 2.5
        b, s, d = x.shape
        xt = x.reshape(b * s, d)
        scores = jax.nn.sigmoid(xt @ gate_w.T)
        top_scores, top_idx = jax.lax.top_k(scores, TOP_K)
        top_scores = top_scores / (jnp.sum(top_scores, axis=-1, keepdims=True) + 1e-20)
        top_scores = top_scores * ROUTED_SCALE
        combine = jnp.sum(jax.nn.one_hot(top_idx, E, dtype=xt.dtype) * top_scores[..., None], axis=1)
        h = jnp.einsum('td,edh->eth', xt, w1)
        u = jnp.einsum('td,edh->eth', xt, w3)
        y = jnp.einsum('eth,ehd->etd', jax.nn.silu(h) * u, w2)
        routed = jnp.einsum('etd,te->td', y, combine)
        shared = jax.nn.silu(xt @ sw1) * (xt @ sw3) @ sw2
        return (routed + shared).reshape(b, s, d)
    x = L0_attn_x
    x = x + _L0_attn_ref(_layernorm(x, axis=-1), L0_attn_CQ_w, L0_attn_CQ_b, L0_attn_CQC_w, L0_attn_CQC_b, L0_attn_CQR_w, L0_attn_CQR_b, L0_attn_CKV_w, L0_attn_CKV_b, L0_attn_CKR_w, L0_attn_CKR_b, L0_attn_CKC_w, L0_attn_CKC_b, L0_attn_CV_w, L0_attn_CV_b, L0_attn_OUT_w, L0_attn_OUT_b)
    x = x + _L0_ffn_ref(_layernorm(x, axis=-1), L0_ffn_gate_w, L0_ffn_w1, L0_ffn_w2, L0_ffn_w3, L0_ffn_sw1, L0_ffn_sw2, L0_ffn_sw3)
    return x

_drawn_inputs = setup_inputs


def setup_inputs(seed=0):
    import zlib

    import numpy as np

    out = dict(_drawn_inputs(seed))
    spreads = {'L0_attn_CQ_b': (0.0, 0.1),
     'L0_attn_CQR_b': (0.0, 0.8),
     'L0_attn_CKV_b': (0.0, 0.8),
     'L0_attn_CKR_b': (0.0, 0.8),
     'L0_attn_CV_b': (0.0, 0.332),
     'L0_attn_OUT_b': (0.0, 0.1)}
    factors = {'L0_attn_CQR_w': 8.0, 'L0_attn_CKV_w': 8.0, 'L0_attn_CKR_w': 8.0, 'L0_attn_CV_w': 7.888}
    for name, (base, spread) in spreads.items():
        noise = np.random.default_rng([zlib.crc32(name.encode()), seed]).standard_normal(out[name].shape)
        drawn = base * np.exp(spread * noise) if base else spread * noise
        out[name] = jnp.asarray(drawn.astype(out[name].dtype))
    for name, factor in factors.items():
        out[name] = (out[name] * factor).astype(out[name].dtype)
    return out
```

```python
import numpy as np
import concourse.bass as bass
from concourse import mybir
from contextlib import ExitStack

B, S, D = 2, 2048, 512
T = B * S
C = 128
NH, HD = 8, 16
E, H = 8, 352
TOP_K, ROUTED_SCALE = 2, 2.5
P = 128
DC = D // P
NT = T // P
TB = S // P
CH = 512
NCH = T // CH
CT = CH // P
QC = S // CH
HC = -(-H // P)
HP = HC * P
HL = H - (HC - 1) * P
G = 4
NG = NH // G
VW = 32
NB = TOP_K * T // P + E
TERMS = [(0, 0), (0, 1), (1, 0), (1, 1), (0, 2), (2, 0)]
KR = len(TERMS) * HD
KM = KR + 3
EPS = 1e-5
NEG = -1e30

fp32, bf16, fp16, i32 = mybir.dt.float32, mybir.dt.bfloat16, mybir.dt.float16, mybir.dt.int32
ALU = mybir.AluOpType
ACT = mybir.ActivationFunctionType
AX = mybir.AxisListType

CONST = {}
_at = 0
for _n, _w in (("ident", P), ("iota_p", P), ("iota_b", NB), ("rev8", NT * E), ("iota_be", NB * E),
               ("token", TOP_K * NT), ("den", P)):
    CONST[_n] = (_at, _at + _w)
    _at += _w
CONST_W = _at
CB = {n: (i * P, (i + 1) * P) for i, n in enumerate(("ident", "mask", "mask_t", "before", "ones"))}


def constants():
    c = np.zeros((P, CONST_W), np.float32)
    put = lambda n, v: c.__setitem__((slice(None), slice(*CONST[n])), v)
    put("ident", np.eye(P))
    put("iota_p", np.arange(P)[None])
    put("iota_b", np.arange(NB)[None])
    put("rev8", np.tile(E - np.arange(E), NT)[None])
    put("iota_be", np.repeat(np.arange(NB), E)[None])
    put("token", np.tile(np.arange(NT) * P, TOP_K)[None] + np.arange(P)[:, None] - T // 2)
    den = np.zeros((P, P), np.float32)
    for j in range(G):
        den[j * VW + HD, j * VW:(j + 1) * VW] = 1
    put("den", den)
    cb = np.zeros((P, 5 * P), np.float32)
    cb[:, 0:P] = np.eye(P)
    cb[:, P:2 * P] = np.where(np.arange(P)[None] > np.arange(P)[:, None], NEG, 0)
    cb[:, 2 * P:3 * P] = np.where(np.arange(P)[:, None] > np.arange(P)[None], NEG, 0)
    cb[:, 3 * P:4 * P] = np.arange(P)[:, None] < np.arange(P)[None]
    cb[:, 4 * P:5 * P] = 1
    inv = 1.0 / 10000.0 ** (np.arange(0, C, 2, dtype=np.float32) / np.float32(C))
    f = np.arange(S, dtype=np.float32)[None] * inv.astype(np.float32)[:, None]
    f = np.concatenate([f, f]).astype(np.float64)
    sin = np.sin(f)
    sin[C // 2:] *= -1
    rope = np.stack([np.cos(f), sin], 1).astype(np.float32)
    return c, cb, rope



def run_steps(eng, count, body, u=2):
    for k in range(u):
        body(k, k)
    with eng.Fori(1, count // u - 1) as m:
        for q in range(u):
            body(m * u + q, 2 * u + q)
    for k in range(count - u, count):
        body(k, k)


def attention_plan():
    chunks = [(0, c) for c in range(QC)] + [(1, c) for c in reversed(range(QC))]
    plan = []
    for s in range(len(chunks) + 3):
        a, b = [], []
        if s < len(chunks):
            g, c = chunks[s]
            for i in range(CT):
                n_keys = (c * CT + i + 1) * P
                for j in range(G):
                    for u in range(-(-n_keys // (2 * CH))):
                        a.append(("A", s, g, c, i, j, u))
        if 0 <= s - 2 < len(chunks):
            g, c = chunks[s - 2]
            last = (c + 1) * CT - 1
            for kt in range(last + 1):
                b += [("B", s - 2, g, c, kt, 0), ("B", s - 2, g, c, kt, 1)]
                if kt:
                    b.append(("PV", s - 2, g, c, kt - 1))
                b += [("B", s - 2, g, c, kt, 2), ("B", s - 2, g, c, kt, 3)]
            b.append(("PV", s - 2, g, c, last))
        stage, done = [], 0
        for x, item in enumerate(b):
            stage.append(item)
            while done < len(a) and done * len(b) < (x + 1) * len(a):
                stage.append(a[done])
                done += 1
        stage += a[done:]
        at = min(6, len(stage))
        if 0 <= s - 3:
            stage.insert(at, ("OT", s - 3, *chunks[s - 3]))
            at = min(at + 6, len(stage))
        if 0 <= s - 1 < len(chunks):
            stage.insert(at if s != 1 else len(stage) // 2, ("TR", s - 1, *chunks[s - 1]))
        if s < len(chunks):
            stage.append(("NP", s, *chunks[s]))
        plan += stage
    return chunks, plan


def program(nc, io):
    ctx = ExitStack()
    with ctx:
        sb = lambda name, shape, dt=fp32: ctx.enter_context(nc.sbuf_tensor(name, shape, dt))
        sem = lambda name: ctx.enter_context(nc.semaphore(name))
        dram = lambda name, shape, dt=fp32: nc.dram_tensor(name, shape, dt, kind="Internal").ap()

        qk_parts = dram("qk_parts", [2, 3, C, T], bf16)
        v_rows = dram("v_rows", [T, NH * VW])
        attn_cols = dram("attn_cols", [C, T])
        xn2_rows = dram("xn2_rows", [T, D])
        base_rows = dram("base_rows", [T, D])
        y_rows = dram("y_rows", [NB * P, D])

        const = sb("const", [P, CONST_W])
        constb = sb("constb", [P, 5 * P], bf16)
        cf = lambda n: const[:, CONST[n][0]:CONST[n][1]]
        cbf = lambda n: constb[:, CB[n][0]:CB[n][1]]
        ident, identb = cf("ident"), cbf("ident")
        out_wt = sb("out_wt", [P, D])
        out_b = sb("out_b", [P, D])
        W13, W2 = DC * 2 * H, HC * D
        SH13 = DC * (2 * H + E)
        sh_at = E * (W13 + W2)
        arena = sb("arena", [P, sh_at + SH13 + W2])
        w13 = arena[:, 0:E * W13].rearrange("p (e c n) -> p e c n", e=E, c=DC)
        w2 = arena[:, E * W13:sh_at].rearrange("p (e c n) -> p e c n", e=E, c=HC)
        sh13 = arena[:, sh_at:sh_at + SH13].rearrange("p (c n) -> p c n", c=DC)
        sh2 = arena[:, sh_at + SH13:].rearrange("p (c n) -> p c n", c=HC)
        cursor = [0]

        def carve(words, dt=fp32):
            a = arena[:, cursor[0]:cursor[0] + words]
            cursor[0] += words
            assert cursor[0] <= sh_at
            return a if dt is fp32 else a.bitcast(dt)

        rope = carve(2 * S).rearrange("p (a n) -> p a n", a=2)
        x_in = [carve(CT * D).rearrange("p (t n) -> p t n", t=CT) for _ in range(2)]
        xn_t = [carve(DC * CH).rearrange("p (c n) -> p c n", c=DC) for _ in range(2)]
        gel = [carve(CH) for _ in range(3)]
        rot = [carve(CH) for _ in range(2)]
        rest = carve(CH)
        parts = [carve(2 * 3 * CH // 2, bf16).rearrange("p (a b n) -> p a b n", a=2, b=3) for _ in range(2)]
        v_out = [carve(CT * NH * VW).rearrange("p (t h w) -> p t h w", t=CT, h=NH) for _ in range(2)]
        w_in = carve(3 * D).rearrange("p (a n) -> p a n", a=3)
        w_t = carve(3 * D).rearrange("p (a c n) -> p a c n", a=3, c=DC)
        cv_w, cv_t = carve(C), carve(C)
        out_w = carve(DC * C).rearrange("p (c n) -> p c n", c=DC)
        gate_w = carve(D)
        constb_in = carve(5 * P)
        cursor[0] = 0
        stack_q = [carve(G * S // 2, bf16).rearrange("p (j n) -> p j n", j=G) for _ in range(NG)]
        stack_k = [carve(G * S // 2, bf16).rearrange("p (j n) -> p j n", j=G) for _ in range(NG)]
        v_sb = [carve(TB * G * VW).rearrange("p (t j w) -> p t j w", t=TB, j=G) for _ in range(NG)]
        PS = 2 * G
        probs = carve(PS * CH).rearrange("p (s n) -> p s n", s=PS)
        o_sb = [carve(CH) for _ in range(2)]
        n_sb = [carve(CH) for _ in range(2)]
        inv_den = carve(CH)
        m_raw = carve(2 * 2 * G * CT).rearrange("p (a u i j) -> p a u i j", a=2, u=2, j=G)
        m_neg, m_rest = (carve(G * CT).rearrange("p (i j) -> p i j", j=G) for _ in range(2))
        m_parts = [carve(3 * G * CT // 2, bf16) for _ in range(2)]
        m_rows = [carve(CH // 2, bf16) for _ in range(2)]

        b_proj = sb("b_proj", [P, 3])
        b_v = sb("b_v", [P, C])
        stats = sb("stats", [P, CT, 6])
        mv = sb("mv", [P, CT, 2])
        rstd, var, newton = (sb(n, [P, CT]) for n in ("rstd", "var", "newton"))
        N_NORM = 14

        attn_cur = sb("attn_cur", [P, 2, P])
        xg = sb("xg", [P, 2, D])
        xg_t = sb("xg_t", [P, 2, DC, P])
        silu = sb("silu", [P, H])
        act_sb = sb("act_sb", [P, 2, HP])
        act_t = sb("act_t", [P, 2, HC, P])
        y_sb = sb("y_sb", [P, 2, D])
        x1 = sb("x1", [P, 4, D])
        logits = sb("logits", [P, NT, E])
        weight = sb("weight", [P, TOP_K * NT])
        slot_i = sb("slot_i", [P, TOP_K * NT], i32)
        idx_i = sb("idx_i", [P, NB], i32)
        cur_i = sb("cur_i", [P, 2], i32)
        cur_s = sb("cur_s", [P, 2 * TOP_K], i32)
        eid_i = sb("eid_i", [1, NB], i32)
        sel_b = sb("sel_b", [P, NT * E], bf16)
        oh_row = sb("oh_row", [P, 2, P], fp16)
        oh_blk = sb("oh_blk", [P, 2, NB], fp16)
        per_e = sb("per_e", [P, 5 * E])
        per_ei = sb("per_ei", [P, E], i32)
        per_s = sb("per_s", [P, 6 * NT])
        slot_f = sb("slot_f", [P, 3, TOP_K * NT])
        slot_t = sb("slot_t", [P, TOP_K * NT], i32)
        eid_f = sb("eid_f", [1, NB])

        psum = ctx.enter_context(nc.psum_tensor("psum", [P, 8, 512], fp32))
        m_bank = psum[0:3 * G, 7, 0:CH // 2].bitcast(bf16)

        s_c = sem("constants_loaded")
        s_cb = sem("bfloat16_constants_ready")
        s_pw = sem("projection_weights_loaded")
        N_PW = 12
        s_wt, s_wte = sem("weights_transposed"), sem("weights_t_ready")
        s_x = [sem(f"x_loaded_{i}") for i in range(2)]
        s_ln = sem("ln_chain")
        s_xn = sem("xn_ready")
        s_xt, s_xte = sem("xn_transposed"), sem("xn_t_ready")
        s_pc, s_pq, s_pk = sem("kv_projected"), sem("q_projected"), sem("k_projected")
        s_gc = sem("kv_gelu_ready")
        s_vp = sem("v_projected")
        s_half = sem("rope_halves_ready")
        s_rope = sem("rope_ready")
        s_gel = sem("qk_gelu_ready")
        s_split = sem("split_chain")
        s_parts = sem("parts_ready")
        s_vout = sem("v_ready")
        s_vpad = sem("v_pad_set")
        s_pst = [sem(f"parts_stored_{i}") for i in range(2)]
        s_kone = sem("k_ones_set")
        s_stack = [sem(f"stacks_loaded_{g}") for g in range(NG)]
        N_STACK = 2 * len(TERMS) + 1
        s_a, s_ar = sem("a_scores_ready"), sem("a_scores_used")
        s_npc, s_np = sem("max_chain"), sem("max_parts_ready")
        s_b, s_e = sem("b_scores_ready"), sem("probs_ready")
        s_pv = sem("pv_groups_done")
        s_oe = sem("chunk_output_copied")
        s_m, s_me = sem("misc_bank_ready"), sem("misc_bank_used")
        s_mld = [sem(f"max_rows_loaded_{i}") for i in range(2)]
        s_att = sem("attention_chunks_ready")
        s_ast = [sem(f"attention_chunks_stored_{i}") for i in range(2)]
        s_w, s_sw = sem("expert_weights_loaded"), sem("shared_weights_loaded")
        s_zero = sem("act_pad_zeroed")

        def pipe(tag):
            names = ("xg_ready", "xt", "xte", "up", "silu", "a", "at", "ate", "dn", "ye", "rows_0", "rows_1",
                     "stored_0", "stored_1")
            return {x: sem(f"{tag}_{x}") for x in names}

        sh, ro = pipe("shared"), pipe("routed")
        s_xr = [sem(f"x_row_loaded_{i}") for i in range(4)]
        s_ac = [sem(f"attention_tile_loaded_{i}") for i in range(2)]
        s_op, s_x1 = sem("out_projected"), sem("x1_ready")
        s_fl = sem("front_chain")
        s_xns = [sem(f"xn2_stored_{i}") for i in range(2)]
        s_lg, s_sig = sem("logits_ready"), sem("sigmoid_ready")
        s_r = sem("route_chain")
        s_sel, s_cnt = sem("selected_ready"), sem("counts_ready")
        s_oh, s_ohp = sem("one_hot_ready"), sem("one_hot_used")
        s_idx = sem("indices_ready")
        s_cur, s_curs = sem("block_indices_copied"), sem("tile_slots_copied")
        s_f = [sem(f"base_rows_loaded_{i}") for i in range(2)]
        s_fg = [sem(f"slots_gathered_{i}") for i in range(2)]
        s_fc, s_fd = sem("first_slot_added"), sem("second_slot_added")
        s_fst = [sem(f"output_stored_{i}") for i in range(2)]

        chunks, plan = attention_plan()
        NS = len(chunks)
        n_a, n_b, n_pv = (sum(x[0] == w for x in plan) for w in ("A", "B", "PV"))
        misc = [x[:2] for x in plan if x[0] in ("TR", "OT")]
        N_MISC = len(misc)
        x_chunk = io["x"].rearrange("(n t p) d -> n p t d", t=CT, p=P)
        rows = lambda a, n: a[bass.ds(n * P, P), :]
        v_tiles = v_rows.rearrange("(t p) w -> p t w", p=P)
        used = lambda n, k: 8 * (n - k % 2)
        used4 = lambda n, k: 4 * (n - k % 4)

        def wait_apart(eng, s, value):
            value = value if isinstance(value, int) else eng.to_reg(value)
            eng.wait_ge(s_c, 32)
            eng.wait_ge(s, value)

        block = ctx.enter_context(nc.Block())

        @block.sync
        def _(sp):
            sp.dma_start(const[:, :], io["const"]).then_inc(s_c, 16)
            sp.dma_start(constb_in, io["constb"]).then_inc(s_c, 16)
            for a, n in enumerate(("wq", "wk", "wc")):
                sp.dma_start(w_in[:, a, :], io[n]).then_inc(s_pw, 16)
            sp.dma_start(cv_w, io["wv"]).then_inc(s_pw, 16)
            sp.dma_start(out_w, io["wo"].rearrange("(c p) n -> p c n", p=P)).then_inc(s_pw, 16)
            sp.dma_start(gate_w[0:E, :], io["gate"]).then_inc(s_pw, 16)
            for a, n in enumerate(("bq", "bk", "bc")):
                sp.dma_start(b_proj[:, a:a + 1], io[n].rearrange("(p a) -> p a", a=1)).then_inc(s_pw, 16)
            sp.dma_start(b_v[:, :], io["bv"].rearrange("(a n) -> a n", a=1).broadcast_to([P, C])).then_inc(s_pw, 16)
            sp.dma_start(out_b[:, :], io["bo"].rearrange("(a n) -> a n", a=1).broadcast_to([P, D])).then_inc(s_pw, 16)
            sp.dma_start(rope, io["rope"]).then_inc(s_pw, 16)

            def load_x(n, k):
                if k >= 2:
                    sp.wait_ge(s_xt, n - 1)
                sp.dma_start(x_in[k % 2], x_chunk[bass.ds(n, 1)].rearrange("a p t d -> p (a t) d")).then_inc(s_x[k % 2], 16)

            def projections(n, k):
                if k < NCH - 2:
                    load_x(n + 2, k + 2)
                sp.wait_ge(s_vout, n + 1)
                sp.dma_start(v_tiles[:, bass.ds(n * CT, CT)],
                             v_out[k % 2].rearrange("p t h w -> p t (h w)")).then_inc(s_pst[k % 2], 16)
                sp.wait_ge(s_parts, 2 * n + 2)
                for a in range(2):
                    sp.dma_start(qk_parts[a][:, :, bass.ds(n * CH, CH)].rearrange("b p n -> p b n"),
                                 parts[k % 2][:, a]).then_inc(s_pst[k % 2], 16)

            load_x(0, 0)
            load_x(1, 1)
            sp.dma_start(sh13[:, :, 0:H], io["sw1"].rearrange("(c p) n -> p c n", p=P)).then_inc(s_sw, 16)
            sp.dma_start(sh13[:, :, H + E:], io["sw3"].rearrange("(c p) n -> p c n", p=P)).then_inc(s_sw, 16)
            sp.dma_start(sh2[:, 0:HC - 1, :], io["sw2"][0:(HC - 1) * P].rearrange("(c p) n -> p c n", p=P)).then_inc(s_sw, 16)
            sp.dma_start(sh2[0:HL, HC - 1, :], io["sw2"][(HC - 1) * P:]).then_inc(s_sw, 16)
            run_steps(sp, NCH, projections)
            for i in range(2):
                sp.wait_ge(s_pst[i], 16 * 3 * NCH // 2)

            with sp.Fori(0, B) as b:
                for g in range(NG):
                    for which, stack in enumerate((stack_q[g], stack_k[g])):
                        for r, term in enumerate(TERMS):
                            src = qk_parts[which, term[which], g * G * HD:(g + 1) * G * HD, bass.ds(b * S, S)]
                            sp.dma_start(stack[r * HD:(r + 1) * HD, :, :],
                                         src.rearrange("(j d) n -> d j n", j=G)).then_inc(s_stack[g], 16)
                    sp.dma_start(v_sb[g].rearrange("p t j w -> p t (j w)"),
                                 v_tiles[:, bass.ds(b * TB, TB), g * G * VW:(g + 1) * G * VW]).then_inc(s_stack[g], 16)
                for s in range(1, NS + 3):
                    if s - 1 < NS:
                        n = s - 1
                        g, c = chunks[n]
                        sp.wait_ge(s_me, b * N_MISC + misc.index(("TR", n)) + 1)
                        sp.dma_start(stack_q[g][KR:KM, :, c * CH:(c + 1) * CH],
                                     m_rows[n % 2][0:3 * G, :]).then_inc(s_mld[n % 2], 16)
                    if s >= 3:
                        n = s - 3
                        g, c = chunks[n]
                        wait_apart(sp, s_att, b * NS + n + 1)
                        for j in range(G):
                            h = (g * G + j) * HD
                            sp.dma_start(attn_cols[h:h + HD, bass.ds(b * S + c * CH, CH)],
                                         n_sb[n % 2][j * VW:j * VW + HD, :]).then_inc(s_ast[n % 2], 16)
                wait_apart(sp, s_pv, (b + 1) * n_pv)
            for i in range(2):
                sp.wait_ge(s_ast[i], 16 * G * B * NS // 2)

            def load_attn(n, k):
                if k >= 2:
                    sp.wait_ge(s_op, n - 1)
                sp.dma_start(attn_cur[:, k % 2, :], attn_cols[:, bass.ds(n * P, P)]).then_inc(s_ac[k % 2], 16)

            def load_row(n, k):
                if k >= 4:
                    sp.wait_ge(sh["ye"], n - 3)
                sp.dma_start(x1[:, k % 4, :], rows(io["x"], n)).then_inc(s_xr[k % 4], 16)

            def store_xn2(n, k):
                sp.wait_ge(sh["xg_ready"], n + 1)
                sp.dma_start(rows(xn2_rows, n), xg[:, k % 2, :]).then_inc(s_xns[k % 2], 16)

            def store_y(ss, dst, n, k):
                sp.wait_ge(ss["ye"], n + 1)
                sp.dma_start(rows(dst, n), y_sb[:, k % 2, :]).then_inc(ss[f"stored_{k % 2}"], 16)

            def shared(n, k):
                if k < NT - 3:
                    load_attn(n + 3, k + 3)
                if k < NT - 2:
                    store_xn2(n + 2, k + 2)
                if k >= 1:
                    store_y(sh, base_rows, n - 1, k - 1)
                if k < NT - 3:
                    load_row(n + 3, k + 3)

            for k in range(3):
                load_row(k, k)
            load_attn(0, 0)
            load_attn(1, 1)
            for e in range(E):
                sp.dma_start(w13[:, e, :, 0:H], io["w1"][e].rearrange("(c p) n -> p c n", p=P)).then_inc(s_w, 16)
                sp.dma_start(w13[:, e, :, H:], io["w3"][e].rearrange("(c p) n -> p c n", p=P)).then_inc(s_w, 16)
                sp.dma_start(w2[:, e, 0:HC - 1, :], io["w2"][e, 0:(HC - 1) * P].rearrange("(c p) n -> p c n", p=P)).then_inc(s_w, 16)
                sp.dma_start(w2[0:HL, e, HC - 1, :], io["w2"][e, (HC - 1) * P:]).then_inc(s_w, 16)
            load_attn(2, 2)
            store_xn2(0, 0)
            store_xn2(1, 1)
            run_steps(sp, NT, shared, 4)
            store_y(sh, base_rows, NT - 1, NT - 1)
            run_steps(sp, NB, lambda n, k: store_y(ro, y_rows, n, k))

            def load_base(n, k):
                if k >= 2:
                    sp.wait_ge(s_fst[k % 2], used(n, k))
                sp.dma_start(xg[:, k % 2, :], rows(base_rows, n)).then_inc(s_f[k % 2], 16)

            def last(n, k):
                sp.wait_ge(s_fd, n + 1)
                sp.dma_start(rows(io["out"], n), xg[:, k % 2, :]).then_inc(s_fst[k % 2], 16)
                if k < NT - 2:
                    load_base(n + 2, k + 2)

            for i in range(2):
                sp.wait_ge(sh[f"stored_{i}"], 16 * NT // 2)
            sp.wait_ge(ro["xt"], NB)
            load_base(0, 0)
            load_base(1, 1)
            run_steps(sp, NT, last)
            for i in range(2):
                sp.wait_ge(s_fst[i], 16 * NT // 2)

        @block.gpsimd
        def _(pool):
            nc.gpsimd.memset(act_sb[:, :, H:], 0.0).then_inc(s_zero, 1)
            for i in range(2):
                nc.gpsimd.memset(v_out[i][:, :, :, HD + 1:], 0.0).then_inc(s_vpad, 1)
                nc.gpsimd.memset(v_out[i][:, :, :, HD:HD + 1], 1.0).then_inc(s_vpad, 1)
            for i in range(2):
                pool.wait_ge(s_pst[i], 16 * 3 * NCH // 2)
            for g in range(NG):
                nc.gpsimd.memset(stack_k[g][KR:KM], 1.0).then_inc(s_kone, 1)

            pool.wait_ge(s_idx, 1)
            for i in range(2):
                pool.wait_ge(s_xns[i], 16 * NT // 2)

            def gather(n, k):
                if k >= 2:
                    pool.wait_ge(ro["xt"], n - 1)
                nc.gpsimd.tensor_copy(cur_i[:, k % 2:k % 2 + 1], idx_i[:, bass.ds(n, 1)]).then_inc(s_cur, 1)
                wait_apart(pool, s_cur, n + 1)
                nc.gpsimd.indirect_dma_start(
                    out=xg[:, k % 2, :], out_offset=None, in_=xn2_rows[:, :],
                    in_offset=bass.IndirectOffsetOnAxis(ap=cur_i[:, k % 2:k % 2 + 1], axis=0),
                ).then_inc(ro[f"rows_{k % 2}"], 16)

            run_steps(pool, NB, gather)
            for i in range(2):
                pool.wait_ge(ro[f"stored_{i}"], 16 * NB // 2)

            def gather_slots(n, k):
                if k >= 2:
                    pool.wait_ge(s_fd, n - 1)
                for q in range(TOP_K):
                    at = TOP_K * (k % 2) + q
                    i = nc.gpsimd.tensor_copy(cur_s[:, at:at + 1], slot_i[:, bass.ds(n + q * NT, 1)])
                i.then_inc(s_curs, 1)
                wait_apart(pool, s_curs, n + 1)
                for q, room in ((0, y_sb), (1, x1)):
                    at = TOP_K * (k % 2) + q
                    nc.gpsimd.indirect_dma_start(
                        out=room[:, k % 2, :], out_offset=None, in_=y_rows[:, :],
                        in_offset=bass.IndirectOffsetOnAxis(ap=cur_s[:, at:at + 1], axis=0),
                    ).then_inc(s_fg[k % 2], 16)

            run_steps(pool, NT, gather_slots)

        @block.scalar
        def _(act):
            act.wait_ge(s_pw, 16 * N_PW)
            for a in range(3):
                act.wait_ge(s_wt, a + 1)
                nc.scalar.copy(w_t[:, a, :, :], psum[:, a, :].rearrange("p (c n) -> p c n", c=DC)).then_inc(s_wte, 1)
            act.wait_ge(s_wt, 4)
            nc.scalar.copy(out_wt[:, :], psum[:, 3, :]).then_inc(s_wte, 1)
            act.wait_ge(s_wt, 6)
            nc.scalar.copy(cv_t, psum[:, 4, 0:C]).then_inc(s_wte, 1)
            nc.scalar.copy(sh13[:, :, H:H + E], psum[:, 4, C:C + DC * E].rearrange("p (c n) -> p c n", c=DC)).then_inc(s_wte, 1)

            def xt_copy(n, k):
                act.wait_ge(s_xt, n + 1)
                if k >= 2:
                    act.wait_ge(s_pk, n - 1)
                for c in range(DC):
                    i = nc.scalar.copy(xn_t[k % 2][:, c, :], psum[:, c, :])
                i.then_inc(s_xte, 1)

            def projections(n, k):
                act.wait_ge(s_pc, n + 1)
                if k >= 1:
                    act.wait_ge(s_vp, n)
                nc.scalar.activation(gel[2], psum[:, 6, :], ACT.Gelu, bias=b_proj[:, 2:3]).then_inc(s_gc, 1)
                if k < NCH - 1:
                    xt_copy(n + 1, k + 1)
                for a in range(2):
                    act.wait_ge(s_rope, 2 * n + a + 1)
                    if k >= 1:
                        act.wait_ge(s_parts, 2 * n - 1 + a)
                    nc.scalar.activation(gel[a], rot[a], ACT.Gelu).then_inc(s_gel, 1)

            xt_copy(0, 0)
            run_steps(act, NCH, projections)

            with act.Fori(0, B) as b:
                at_b = at_pv = 0
                for item in plan:
                    if item[0] == "B":
                        _, n, g, c, kt, j = item
                        d = max(kt - c * CT, 0)
                        act.wait_ge(s_b, b * n_b + at_b + 1)
                        if at_b >= PS:
                            act.wait_ge(s_pv, b * n_pv + at_b // G - 1)
                        nc.scalar.activation(probs[:, at_b % PS, d * P:], psum[:, 4 + at_b % 2, 0:CH - d * P], ACT.Exp,
                                             scale=float(HD) ** -0.5).then_inc(s_e, 1)
                        at_b += 1
                    if item[0] == "PV":
                        _, n, g, c, kt = item
                        at_pv += 1
                        if kt == (c + 1) * CT - 1:
                            act.wait_ge(s_pv, b * n_pv + at_pv)
                            if n >= 2:
                                act.wait_ge(s_att, b * NS + n - 1)
                            nc.scalar.copy(o_sb[n % 2], psum[:, 6, :]).then_inc(s_oe, 1)
                act.wait_ge(s_pv, (b + 1) * n_pv)
                act.wait_ge(s_att, (b + 1) * NS)

            def experts(ss, count, u):
                def xt_copy(n, k):
                    act.wait_ge(ss["xt"], n + 1)
                    if k >= 2:
                        act.wait_ge(ss["up"], n - 1)
                    nc.scalar.copy(xg_t[:, k % 2], psum[:, 0, :].rearrange("p (c n) -> p c n", c=DC)).then_inc(ss["xte"], 1)

                def at_copy(n, k):
                    act.wait_ge(ss["at"], n + 1)
                    if k >= 2:
                        act.wait_ge(ss["dn"], n - 1)
                    nc.scalar.copy(act_t[:, k % 2], psum[:, 5, 0:HP].rearrange("p (c n) -> p c n", c=HC)).then_inc(ss["ate"], 1)

                def step(n, k):
                    if k < count - 1:
                        xt_copy(n + 1, k + 1)
                    if k >= 1:
                        at_copy(n - 1, k - 1)
                    act.wait_ge(ss["up"], n + 1)
                    if k >= 1:
                        act.wait_ge(ss["a"], n)
                    nc.scalar.activation(silu[:, :], psum[:, 1 + k % 2, 0:H], ACT.Silu).then_inc(ss["silu"], 1)

                xt_copy(0, 0)
                run_steps(act, count, step, u)
                at_copy(count - 1, count - 1)

            experts(sh, NT, 4)
            act.wait_ge(s_lg, NT)
            nc.scalar.activation(logits[:, :, :], logits[:, :, :], ACT.Sigmoid).then_inc(s_sig, 1)
            experts(ro, NB, 2)

        @block.tensor
        def _(pe):
            pe.wait_ge(s_c, 32)
            pe.wait_ge(s_pw, 16 * N_PW)
            for a in range(3):
                for c in range(DC):
                    i = nc.tensor.transpose(psum[:, a, c * P:(c + 1) * P], w_in[:, a, c * P:(c + 1) * P], ident)
                i.then_inc(s_wt, 1)
            for c in range(DC):
                i = nc.tensor.transpose(psum[:, 3, c * P:(c + 1) * P], out_w[:, c, :], ident)
            i.then_inc(s_wt, 1)
            nc.tensor.transpose(psum[:, 4, 0:C], cv_w, ident).then_inc(s_wt, 1)
            for c in range(DC):
                i = nc.tensor.transpose(psum[:, 4, C + c * E:C + (c + 1) * E], gate_w[0:E, c * P:(c + 1) * P], ident[0:E, 0:E])
            i.then_inc(s_wt, 1)

            def transposes(n, k):
                pe.wait_ge(s_xn, n + 1)
                if k >= 1:
                    pe.wait_ge(s_xte, n)
                for c in range(DC):
                    for t in range(CT):
                        i = nc.tensor.transpose(psum[:, c, t * P:(t + 1) * P], x_in[k % 2][:, t, c * P:(c + 1) * P], ident)
                i.then_inc(s_xt, 1)

            def projections(n, k):
                pe.wait_ge(s_xte, n + 1)
                for which, bank, done in ((2, 6, s_pc), (0, 4, s_pq), (1, 5, s_pk)):
                    if k >= 1 and which == 2:
                        pe.wait_ge(s_gc, n)
                    elif k >= 1:
                        pe.wait_ge(s_rope, 2 * n - 1 + which)
                    for c in range(DC):
                        i = nc.tensor.matmul(psum[:, bank, :], w_t[:, which, c, :], xn_t[k % 2][:, c, :],
                                             start=c == 0, stop=c == DC - 1)
                    i.then_inc(done, 1)
                if k < NCH - 1:
                    transposes(n + 1, k + 1)
                pe.wait_ge(s_gc, n + 1)
                if k >= 1:
                    pe.wait_ge(s_vout, n)
                for t in range(CT):
                    i = nc.tensor.matmul(psum[:, 7, t * P:(t + 1) * P], gel[2][:, t * P:(t + 1) * P], cv_t, start=True, stop=True)
                i.then_inc(s_vp, 1)

            pe.wait_ge(s_wte, 6)
            transposes(0, 0)
            run_steps(pe, NCH, projections)

            pe.wait_ge(s_kone, NG)
            pe.wait_ge(s_cb, 1)
            pe.wait_ge(s_vout, NCH)
            pe.wait_ge(s_rope, 2 * NCH)
            with pe.Fori(0, B) as b:
                at_a = at_b = at_pv = at_m = 0
                for item in plan:
                    if item[0] == "A":
                        _, n, g, c, i, j, u = item
                        if i == j == u == 0:
                            pe.wait_ge(s_stack[g], (b + 1) * (16 * N_STACK))
                        qt = c * CT + i
                        if at_a >= 2:
                            pe.wait_ge(s_ar, b * n_a + at_a - 1)
                        bank = 2 * (at_a % 2)
                        end = min(2 * CH * (u + 1), (qt + 1) * P)
                        for k0 in range(2 * CH * u, end, CH):
                            w = min(CH, end - k0)
                            diagonal = k0 + w == (qt + 1) * P
                            ins = nc.tensor.matmul(psum[:, bank, 0:w], stack_q[g][0:KR, j, qt * P:(qt + 1) * P],
                                                   stack_k[g][0:KR, j, k0:k0 + w], start=True, stop=not diagonal)
                            if diagonal:
                                ins = nc.tensor.matmul(psum[:, bank, w - P:w], identb, cbf("mask"), start=False, stop=True)
                            bank += 1
                        ins.then_inc(s_a, 1)
                        at_a += 1
                    if item[0] == "B":
                        _, n, g, c, kt, j = item
                        if kt == j == 0:
                            pe.wait_ge(s_mld[n % 2], b * (16 * NS // 2) + 16 * (n // 2 + 1))
                        d = max(kt - c * CT, 0)
                        if at_b >= 2:
                            pe.wait_ge(s_e, b * n_b + at_b - 1)
                        bank = 4 + at_b % 2
                        diagonal = kt >= c * CT
                        ins = nc.tensor.matmul(psum[:, bank, 0:CH - d * P], stack_k[g][0:KM, j, kt * P:(kt + 1) * P],
                                               stack_q[g][0:KM, j, c * CH + d * P:(c + 1) * CH], start=True, stop=not diagonal)
                        if diagonal:
                            ins = nc.tensor.matmul(psum[:, bank, 0:P], identb, cbf("mask_t"), start=False, stop=True)
                        ins.then_inc(s_b, 1)
                        at_b += 1
                    if item[0] == "PV":
                        _, n, g, c, kt = item
                        last = (c + 1) * CT - 1
                        d = max(kt - c * CT, 0)
                        if kt == 0 and n >= 1:
                            pe.wait_ge(s_oe, b * NS + n)
                        pe.wait_ge(s_e, b * n_b + (at_pv + 1) * G)
                        for j in range(G):
                            ins = nc.tensor.matmul(psum[VW * j:VW * (j + 1), 6, d * P:], v_sb[g][:, kt, j, :],
                                                   probs[:, (at_pv * G + j) % PS, d * P:], start=kt == 0, stop=kt == last)
                        ins.then_inc(s_pv, 1)
                        at_pv += 1
                    if item[0] in ("TR", "OT"):
                        n = item[1]
                        if at_m >= 1:
                            pe.wait_ge(s_me, b * N_MISC + at_m)
                        at_m += 1
                    if item[0] == "TR":
                        pe.wait_ge(s_np, b * NS + n + 1)
                        for i in range(CT):
                            ins = nc.tensor.transpose(m_bank[:, i * P:(i + 1) * P], m_parts[n % 2][:, i * 3 * G:(i + 1) * 3 * G], identb)
                        ins.then_inc(s_m, 1)
                    if item[0] == "OT":
                        pe.wait_ge(s_oe, b * NS + n + 1)
                        nc.tensor.matmul(psum[:, 7, :], cf("den"), o_sb[n % 2], start=True, stop=True).then_inc(s_m, 1)
                pe.wait_ge(s_ar, (b + 1) * n_a)
                pe.wait_ge(s_e, (b + 1) * n_b)
                pe.wait_ge(s_oe, (b + 1) * NS)
                pe.wait_ge(s_me, (b + 1) * N_MISC)

            def experts(ss, count, shared, u):
                def front(n, k):
                    pe.wait_ge(s_ac[k % 2], used(n, k) + 16)
                    if k >= 1:
                        pe.wait_ge(s_x1, n)
                    nc.tensor.matmul(psum[:, 7, :], attn_cur[:, k % 2, :], out_wt[:, :], start=True, stop=True).then_inc(s_op, 1)

                def xt(n, k):
                    if shared:
                        pe.wait_ge(ss["xg_ready"], n + 1)
                    else:
                        pe.wait_ge(ss[f"rows_{k % 2}"], used(n, k) + 16)
                    if k >= 1:
                        pe.wait_ge(ss["xte"], n)
                    for c in range(DC):
                        i = nc.tensor.transpose(psum[:, 0, c * P:(c + 1) * P], xg[:, k % 2, c * P:(c + 1) * P], ident)
                    i.then_inc(ss["xt"], 1)

                def at(n, k):
                    pe.wait_ge(ss["a"], n + 1)
                    if k >= 1:
                        pe.wait_ge(ss["ate"], n)
                    for c in range(HC):
                        i = nc.tensor.transpose(psum[:, 5, c * P:(c + 1) * P], act_sb[:, k % 2, c * P:(c + 1) * P], ident)
                    i.then_inc(ss["at"], 1)

                def up(n, k, e):
                    pe.wait_ge(ss["xte"], n + 1)
                    if k >= 2:
                        pe.wait_ge(ss["a"], n - 1)
                        if shared:
                            pe.wait_ge(s_lg, n - 1)
                    for q, bank in enumerate((1, 3)):
                        for c in range(DC):
                            if shared:
                                rhs = sh13[:, c, (0, H + E)[q]:(H + E, 2 * H + E)[q]]
                            else:
                                rhs = w13[:, bass.ds(e, 1), c, q * H:(q + 1) * H].rearrange("p a n -> p (a n)")
                            w = H + E if shared and q == 0 else H
                            i = nc.tensor.matmul(psum[:, bank + k % 2, 0:w], xg_t[:, k % 2, c, :], rhs, start=c == 0, stop=c == DC - 1)
                    i.then_inc(ss["up"], 1)

                def down(n, k, e):
                    pe.wait_ge(ss["ate"], n + 1)
                    if k >= 1:
                        pe.wait_ge(ss["ye"], n)
                    for c in range(HC):
                        r = P if c < HC - 1 else HL
                        rhs = sh2[0:r, c, :] if shared else w2[0:r, bass.ds(e, 1), c, :].rearrange("p a n -> p (a n)")
                        i = nc.tensor.matmul(psum[:, 6, :], act_t[0:r, k % 2, c, :], rhs, start=c == 0, stop=c == HC - 1)
                    i.then_inc(ss["dn"], 1)

                def expert(n):
                    return None if shared else pe.value_load(eid_i[0:1, bass.ds(n, 1)], min_val=0, max_val=E - 1)

                def step(n, k):
                    if shared and k < count - 2:
                        front(n + 2, k + 2)
                    if k < count - 1:
                        xt(n + 1, k + 1)
                    if k >= 1:
                        at(n - 1, k - 1)
                    up(n, k, expert(n))
                    if k >= 1:
                        down(n - 1, k - 1, expert(n - 1))

                if shared:
                    front(0, 0)
                    front(1, 1)
                xt(0, 0)
                run_steps(pe, count, step, u)
                at(count - 1, count - 1)
                down(count - 1, count - 1, expert(count - 1))

            pe.wait_ge(s_sw, 16 * 4)
            experts(sh, NT, True, 4)
            pe.wait_ge(s_sel, 1)
            nc.tensor.matmul(psum[:, 7, 0:NT * E], cbf("before"), sel_b[:, :], start=True, stop=True)
            nc.tensor.matmul(psum[:, 7, NT * E:], cbf("ones"), sel_b[:, :], start=True, stop=True).then_inc(s_cnt, 1)

            def one_hot(n, k):
                pe.wait_ge(s_oh, n + 1)
                nc.tensor.matmul(psum[:, 0, 0:NB], oh_row[:, k % 2, :], oh_blk[:, k % 2, :],
                                 start=isinstance(n, int) and n == 0, stop=k == TOP_K * NT - 1).then_inc(s_ohp, 1)

            run_steps(pe, TOP_K * NT, one_hot)
            pe.wait_ge(s_idx, 1)
            pe.wait_ge(s_w, 16 * 4 * E)
            experts(ro, NB, False, 2)

        @block.vector
        def _(dve):
            def link(ins, s, value):
                ins.then_inc(s, 1)
                dve.wait_ge(s, value)

            def norm_stats(tiles, s, at):
                for t, x in enumerate(tiles):
                    i = nc.vector.bn_stats(stats[:, t, :], x)
                i.then_inc(s, 1)
                wait_apart(dve, s, at + 1)
                for t in range(len(tiles)):
                    i = nc.vector.bn_aggr(mv[:, t, :], stats[:, t, :])
                link(i, s, at + 2)
                m = len(tiles)
                v, y, t = var[:, 0:m], rstd[:, 0:m], newton[:, 0:m]
                link(nc.vector.tensor_scalar(v, mv[:, 0:m, 1], EPS, None, ALU.add), s, at + 3)
                link(nc.vector.tensor_scalar(t.bitcast(i32), v.bitcast(i32), 1, None, ALU.arith_shift_right), s, at + 4)
                link(nc.vector.tensor_scalar(y.bitcast(i32), t.bitcast(i32), -1.0, float(0x5f3759df), ALU.mult, ALU.add), s, at + 5)
                for i in range(3):
                    link(nc.vector.scalar_tensor_tensor(t, y, -0.5, y, ALU.mult, ALU.mult), s, at + 6 + 3 * i)
                    link(nc.vector.tensor_tensor(t, t, v, ALU.mult), s, at + 7 + 3 * i)
                    link(nc.vector.scalar_tensor_tensor(y, t, 1.5, y, ALU.add, ALU.mult), s, at + 8 + 3 * i)

            def norm(n, k):
                dve.wait_ge(s_x[k % 2], used(n, k) + 16)
                if k >= 1:
                    dve.wait_ge(s_xn, n)
                norm_stats([x_in[k % 2][:, t, :] for t in range(CT)], s_ln, N_NORM * n)
                for t in range(CT):
                    i = nc.vector.tensor_scalar(x_in[k % 2][:, t, :], x_in[k % 2][:, t, :], mv[:, t, 0:1], rstd[:, t:t + 1],
                                                ALU.subtract, ALU.mult)
                i.then_inc(s_xn, 1)

            def projections(n, k):
                if k < NCH - 1:
                    norm(n + 1, k + 1)
                at = bass.ds(n % QC * CH, CH)
                half = C // 2
                for a, (bank, done) in enumerate(((4, s_pq), (5, s_pk))):
                    dve.wait_ge(done, n + 1)
                    if a == 1:
                        dve.wait_ge(s_rope, 2 * n + 1)
                    elif k >= 1:
                        dve.wait_ge(s_parts, 2 * n)
                    if k >= 1:
                        dve.wait_ge(s_gel, 2 * n - 1 + a)
                    nc.vector.scalar_tensor_tensor(rot[a], psum[:, bank, :], b_proj[:, a:a + 1], rope[:, 0, at], ALU.add, ALU.mult)
                    nc.vector.scalar_tensor_tensor(rest[0:half, :], psum[half:C, bank, :], b_proj[half:C, a:a + 1],
                                                   rope[half:C, 1, at], ALU.add, ALU.mult)
                    link(nc.vector.scalar_tensor_tensor(rest[half:C, :], psum[0:half, bank, :], b_proj[0:half, a:a + 1],
                                                        rope[0:half, 1, at], ALU.add, ALU.mult), s_half, 2 * n + a + 1)
                    nc.vector.tensor_tensor(rot[a], rot[a], rest, ALU.add).then_inc(s_rope, 1)
                dve.wait_ge(s_vp, n + 1)
                if k >= 2:
                    dve.wait_ge(s_pst[k % 2], 3 * used(n, k))
                for t in range(CT):
                    i = nc.vector.tensor_tensor(v_out[k % 2][:, t, :, 0:HD],
                                                psum[:, 7, t * P:(t + 1) * P].rearrange("p (h w) -> p h w", h=NH),
                                                b_v[:, :].rearrange("p (h w) -> p h w", h=NH), ALU.add)
                i.then_inc(s_vout, 1)
                for a in range(2):
                    dve.wait_ge(s_gel, 2 * n + a + 1)
                    if a == 0:
                        dve.wait_ge(s_rope, 2 * n + 2)
                    else:
                        dve.wait_ge(s_parts, 2 * n + 1)
                    pt = parts[k % 2]
                    link(nc.vector.tensor_copy(pt[:, a, 0, :], gel[a]), s_split, 6 * n + 3 * a + 1)
                    link(nc.vector.tensor_tensor(rest, gel[a], pt[:, a, 0, :], ALU.subtract), s_split, 6 * n + 3 * a + 2)
                    link(nc.vector.tensor_copy(pt[:, a, 1, :], rest), s_split, 6 * n + 3 * a + 3)
                    nc.vector.tensor_tensor(pt[:, a, 2, :], rest, pt[:, a, 1, :], ALU.subtract).then_inc(s_parts, 1)

            dve.wait_ge(s_c, 32)
            nc.vector.tensor_copy(constb[:, :], constb_in).then_inc(s_cb, 1)
            dve.wait_ge(s_pw, 16 * N_PW)
            dve.wait_ge(s_vpad, 4)
            norm(0, 0)
            run_steps(dve, NCH, projections)
            for i in range(2):
                dve.wait_ge(s_pst[i], 16 * 3 * NCH // 2)

            with dve.Fori(0, B) as b:
                at_a = at_m = links = 0
                n_links = 4 * NS
                for item in plan:
                    if item[0] == "A":
                        _, n, g, c, i, j, u = item
                        w = min(2 * CH, (c * CT + i + 1) * P - 2 * CH * u)
                        dve.wait_ge(s_a, b * n_a + at_a + 1)
                        bank = 2 * (at_a % 2)
                        src = psum[:, bank:bank + 2, :].rearrange("p a n -> p (a n)")[:, 0:w]
                        nc.vector.tensor_reduce(m_raw[:, n % 2, u, i, j:j + 1], src, AX.X, ALU.max).then_inc(s_ar, 1)
                        at_a += 1
                    if item[0] == "NP":
                        _, n, g, c = item
                        dve.wait_ge(s_ar, b * n_a + at_a)
                        raw = [m_raw[:, n % 2, u] for u in range(2)]
                        mp = m_parts[n % 2].rearrange("p (i a j) -> p a i j", a=3, j=G)
                        at = b * n_links + links
                        if c >= QC // 2:
                            link(nc.vector.tensor_tensor(m_neg, raw[0], raw[1], ALU.max), s_npc, at + 1)
                        else:
                            link(nc.vector.tensor_copy(m_neg, raw[0]), s_npc, at + 1)
                        link(nc.vector.tensor_scalar(mp[:, 0], m_neg, -1.0, None, ALU.mult), s_npc, at + 2)
                        link(nc.vector.scalar_tensor_tensor(m_rest, m_neg, -1.0, mp[:, 0], ALU.mult, ALU.subtract), s_npc, at + 3)
                        link(nc.vector.tensor_copy(mp[:, 1], m_rest), s_npc, at + 4)
                        nc.vector.tensor_tensor(mp[:, 2], m_rest, mp[:, 1], ALU.subtract).then_inc(s_np, 1)
                        links += 4
                    if item[0] in ("TR", "OT"):
                        n = item[1]
                        dve.wait_ge(s_m, b * N_MISC + at_m + 1)
                        at_m += 1
                    if item[0] == "TR":
                        if n >= 2:
                            dve.wait_ge(s_mld[n % 2], b * (16 * NS // 2) + 16 * (n // 2))
                        nc.vector.tensor_copy(m_rows[n % 2][0:3 * G, :], m_bank).then_inc(s_me, 1)
                    if item[0] == "OT":
                        if n >= 1:
                            dve.wait_ge(s_att, b * NS + n)
                        link(nc.vector.reciprocal(inv_den, psum[:, 7, :]), s_me, b * N_MISC + at_m)
                        if n >= 2:
                            dve.wait_ge(s_ast[n % 2], b * (16 * G * NS // 2) + 16 * G * (n // 2))
                        nc.vector.tensor_tensor(n_sb[n % 2], o_sb[n % 2], inv_den, ALU.mult).then_inc(s_att, 1)
                dve.wait_ge(s_att, (b + 1) * NS)
                for i in range(2):
                    dve.wait_ge(s_mld[i], (b + 1) * (16 * NS // 2))
                    dve.wait_ge(s_ast[i], (b + 1) * (16 * G * NS // 2))

            dve.wait_ge(s_zero, 1)

            def experts(ss, count, shared, u):
                def front(n, k):
                    row = x1[:, k % 4, :]
                    dve.wait_ge(s_op, n + 1)
                    dve.wait_ge(s_xr[k % 4], used4(n, k) + 16)
                    link(nc.vector.tensor_tensor(row, row, psum[:, 7, :], ALU.add), s_x1, n + 1)
                    link(nc.vector.tensor_tensor(row, row, out_b[:, :], ALU.add), s_fl, (N_NORM + 1) * n + 1)
                    norm_stats([row], s_fl, (N_NORM + 1) * n + 1)
                    if k >= 2:
                        dve.wait_ge(ss["xt"], n - 1)
                        dve.wait_ge(s_xns[k % 2], used(n, k))
                    nc.vector.tensor_scalar(xg[:, k % 2, :], row, mv[:, 0, 0:1], rstd[:, 0:1],
                                            ALU.subtract, ALU.mult).then_inc(ss["xg_ready"], 1)

                def gated(n, k):
                    dve.wait_ge(ss["silu"], n + 1)
                    if k >= 2:
                        dve.wait_ge(ss["at"], n - 1)
                    nc.vector.tensor_tensor(act_sb[:, k % 2, 0:H], psum[:, 3 + k % 2, 0:H], silu[:, :], ALU.mult).then_inc(ss["a"], 1)
                    if shared:
                        nc.vector.tensor_copy(logits[:, bass.ds(n, 1), :].rearrange("p a e -> p (a e)"),
                                              psum[:, 1 + k % 2, H:H + E]).then_inc(s_lg, 1)

                def y(n, k):
                    dve.wait_ge(ss["dn"], n + 1)
                    if k >= 2:
                        dve.wait_ge(ss[f"stored_{k % 2}"], used(n, k))
                    if shared:
                        i = nc.vector.tensor_tensor(y_sb[:, k % 2, :], x1[:, k % 4, :], psum[:, 6, :], ALU.add)
                    else:
                        i = nc.vector.tensor_copy(y_sb[:, k % 2, :], psum[:, 6, :])
                    i.then_inc(ss["ye"], 1)

                def step(n, k):
                    if shared and k < count - 2:
                        front(n + 2, k + 2)
                    gated(n, k)
                    if k >= 1:
                        y(n - 1, k - 1)

                if shared:
                    front(0, 0)
                    front(1, 1)
                run_steps(dve, count, step, u)
                y(count - 1, count - 1)

            experts(sh, NT, True, 4)
            for i in range(2):
                dve.wait_ge(sh[f"stored_{i}"], 16 * NT // 2)
            r_at = [0]

            def step(ins):
                r_at[0] += 1
                link(ins, s_r, r_at[0])

            x1f = x1[:, :, :].rearrange("p a n -> p (a n)")
            te = lambda i: x1f[:, i * NT * E:(i + 1) * NT * E].rearrange("p (t e) -> p t e", e=E)
            over_e = lambda a: a.rearrange("p (t a) -> p t a", a=1).broadcast_to([P, NT, E])
            first, second, left, work, tile_total, before = (te(i) for i in range(6))
            rev = cf("rev8").rearrange("p (t e) -> p t e", e=E)
            top = [per_s[:, i * NT:(i + 1) * NT] for i in range(2)]
            pick, total, inv = (per_s[:, i * NT:(i + 1) * NT] for i in (2, 3, 4))
            dve.wait_ge(s_sig, 1)
            for q, (chosen, scores) in enumerate(((first, logits[:, :, :]), (second, left))):
                step(nc.vector.tensor_reduce(top[q], scores, AX.X, ALU.max))
                step(nc.vector.tensor_tensor(work, scores, over_e(top[q]), ALU.is_equal))
                step(nc.vector.tensor_tensor(work, work, rev, ALU.mult))
                step(nc.vector.tensor_reduce(pick, work, AX.X, ALU.max))
                step(nc.vector.tensor_tensor(chosen, rev, over_e(pick), ALU.is_equal))
                if q == 0:
                    step(nc.vector.scalar_tensor_tensor(left, first, -2.0, logits[:, :, :], ALU.mult, ALU.add))
            nc.vector.tensor_tensor(sel_b[:, :].rearrange("p (t e) -> p t e", e=E), first, second, ALU.add).then_inc(s_sel, 1)
            step(nc.vector.tensor_tensor(total, top[0], top[1], ALU.add))
            step(nc.vector.tensor_scalar(total, total, 1e-20, None, ALU.add))
            step(nc.vector.reciprocal(inv, total))
            for q in range(TOP_K):
                step(nc.vector.tensor_tensor(weight[:, q * NT:(q + 1) * NT], top[q], inv, ALU.mult))
            step(nc.vector.tensor_scalar(weight[:, :], weight[:, :], ROUTED_SCALE, None, ALU.mult))
            dve.wait_ge(s_cnt, 1)
            step(nc.vector.tensor_copy(tile_total.rearrange("p t e -> p (t e)"), psum[:, 7, NT * E:]))
            nc.vector.memset(work, 0.0).then_inc(s_r, 1)
            r_at[0] += 1
            dve.wait_ge(s_r, r_at[0])
            for e in range(E):
                i = nc.vector.tensor_tensor_scan(before[:, :, e], tile_total[:, :, e], work[:, :, e], 0.0, ALU.add, ALU.add)
            step(i)
            count, blocks, ends, base, spare = (per_e[:, i * E:(i + 1) * E] for i in range(5))
            step(nc.vector.tensor_scalar(per_ei[:, :], before[:, NT - 1, :], float(P - 1), None, ALU.add))
            step(nc.vector.tensor_scalar(per_ei[:, :], per_ei[:, :], P.bit_length() - 1, None, ALU.arith_shift_right))
            step(nc.vector.tensor_copy(blocks, per_ei[:, :]))
            step(nc.vector.tensor_tensor_scan(ends, blocks, work[:, 0, :], 0.0, ALU.add, ALU.add))
            step(nc.vector.tensor_tensor(base, ends, blocks, ALU.subtract))
            step(nc.vector.tensor_scalar(base, base, float(P), None, ALU.mult))
            step(nc.vector.tensor_tensor(before, before, tile_total, ALU.subtract))
            step(nc.vector.tensor_tensor(before, before, psum[:, 7, 0:NT * E].rearrange("p (t e) -> p t e", e=E), ALU.add))
            step(nc.vector.tensor_tensor(before, before, base.rearrange("p (a e) -> p a e", a=1).broadcast_to([P, NT, E]), ALU.add))
            for q, chosen in enumerate((first, second)):
                step(nc.vector.tensor_tensor(work, chosen, before, ALU.mult))
                step(nc.vector.tensor_reduce(slot_f[:, 0, q * NT:(q + 1) * NT], work, AX.X, ALU.add))
            step(nc.vector.tensor_copy(slot_i[:, :], slot_f[:, 0, :]))
            step(nc.vector.tensor_scalar(slot_t[:, :], slot_i[:, :], P.bit_length() - 1, None, ALU.arith_shift_right))
            step(nc.vector.tensor_copy(slot_f[:, 2, :], slot_t[:, :]))
            step(nc.vector.scalar_tensor_tensor(slot_f[:, 1, :], slot_f[:, 2, :], -float(P), slot_f[:, 0, :], ALU.mult, ALU.add))
            be = x1f[0:1, 0:NB * E].rearrange("p (b e) -> p b e", e=E)
            step(nc.vector.tensor_tensor(be, ends[0:1, :].rearrange("p (a e) -> p a e", a=1).broadcast_to([1, NB, E]),
                                         cf("iota_be")[0:1, :].rearrange("p (b e) -> p b e", e=E), ALU.is_le))
            step(nc.vector.tensor_reduce(eid_f[:, :], be, AX.X, ALU.add))
            step(nc.vector.tensor_scalar(eid_i[:, :], eid_f[:, :], float(E - 1), None, ALU.min))

            def one_hot(n, k):
                if k >= 2:
                    dve.wait_ge(s_ohp, n - 1)
                col = bass.ds(n, 1)
                nc.vector.tensor_scalar(oh_row[:, k % 2, :], cf("iota_p"), slot_f[:, 1, col], None, ALU.is_equal)
                nc.vector.tensor_scalar(oh_blk[:, k % 2, :], cf("iota_b"), slot_f[:, 2, col], cf("token")[:, col],
                                        ALU.is_equal, ALU.mult).then_inc(s_oh, 1)

            run_steps(dve, TOP_K * NT, one_hot)
            dve.wait_ge(s_ohp, TOP_K * NT)
            nc.vector.tensor_scalar(idx_i[:, :], psum[:, 0, 0:NB], float(T // 2), None, ALU.add).then_inc(s_idx, 1)
            experts(ro, NB, False, 2)

            def last(n, k):
                dve.wait_ge(s_f[k % 2], used(n, k) + 16)
                dve.wait_ge(s_fg[k % 2], 2 * used(n, k) + 32)
                row = xg[:, k % 2, :]
                link(nc.vector.scalar_tensor_tensor(row, y_sb[:, k % 2, :], weight[:, bass.ds(n, 1)], row, ALU.mult, ALU.add), s_fc, n + 1)
                nc.vector.scalar_tensor_tensor(row, x1[:, k % 2, :], weight[:, bass.ds(n + NT, 1)], row, ALU.mult, ALU.add).then_inc(s_fd, 1)

            run_steps(dve, NT, last)


_INS = {"L0_attn_x": "x", "L0_attn_CQR_w": "wq", "L0_attn_CQR_b": "bq", "L0_attn_CKR_w": "wk", "L0_attn_CKR_b": "bk",
        "L0_attn_CKV_w": "wc", "L0_attn_CKV_b": "bc", "L0_attn_CV_w": "wv", "L0_attn_CV_b": "bv", "L0_attn_OUT_w": "wo",
        "L0_attn_OUT_b": "bo", "L0_ffn_gate_w": "gate", "L0_ffn_w1": "w1", "L0_ffn_w2": "w2", "L0_ffn_w3": "w3",
        "L0_ffn_sw1": "sw1", "L0_ffn_sw2": "sw2", "L0_ffn_sw3": "sw3"}


def kernel(**inputs):
    import concourse.bacc as bacc
    from concourse.bass_utils import run_bass_kernel_spmd

    nc = bacc.Bacc("TRN2", target_bir_lowering=False, num_devices=1)
    arrays = {short: np.ascontiguousarray(inputs[name]) for name, short in _INS.items()}
    arrays["x"] = arrays["x"].reshape(T, D)
    arrays["const"], arrays["constb"], arrays["rope"] = constants()
    io = {n: nc.dram_tensor(f"in_{n}", a.shape, mybir.dt.from_np(a.dtype), kind="ExternalInput").ap() for n, a in arrays.items()}
    io["out"] = nc.dram_tensor("out_rows", [T, D], fp32, kind="ExternalOutput").ap()
    program(nc, io)
    r = run_bass_kernel_spmd(nc, [{f"in_{n}": a for n, a in arrays.items()}], core_ids=[0])
    return r.results[0]["out_rows"].reshape(B, S, D)
```

```python
import numpy as np
import concourse.bass as bass
from concourse import mybir
from contextlib import ExitStack

B, S, D = 2, 2048, 512
T = B * S
C = 128
NH, HD = 8, 16
E, H = 8, 352
TOP_K, ROUTED_SCALE = 2, 2.5
P = 128
DC = D // P
NT = T // P
TB = S // P
CH = 512
NCH = T // CH
CT = CH // P
QC = S // CH
HC = -(-H // P)
HP = HC * P
HL = H - (HC - 1) * P
G = 4
NG = NH // G
VW = 32
NB = TOP_K * T // P + E - 1
TERMS = [(0, 0), (0, 1), (1, 0), (1, 1), (0, 2), (2, 0)]
KR = len(TERMS) * HD
KM = KR + 3
N_RC = 4
EPS = 1e-5
NEG = -1e30

fp32, bf16, fp16, i32 = mybir.dt.float32, mybir.dt.bfloat16, mybir.dt.float16, mybir.dt.int32
ALU = mybir.AluOpType
ACT = mybir.ActivationFunctionType
AX = mybir.AxisListType

CONST = {}
_at = 0
for _n, _w in (("ident", P), ("iota_p", P), ("iota_b", NB), ("rev8", NT * E), ("iota_be", NB * E),
               ("token", TOP_K * NT), ("spare_row", 1), ("den", P)):
    CONST[_n] = (_at, _at + _w)
    _at += _w
CONST_W = _at
CB = {n: (i * P, (i + 1) * P) for i, n in enumerate(("ident", "mask", "mask_t", "before", "ones"))}


def constants():
    c = np.zeros((P, CONST_W), np.float32)
    put = lambda n, v: c.__setitem__((slice(None), slice(*CONST[n])), v)
    put("ident", np.eye(P))
    put("iota_p", np.arange(P)[None])
    put("iota_b", np.arange(NB)[None])
    put("rev8", np.tile(E - np.arange(E), NT)[None])
    put("iota_be", np.repeat(np.arange(NB), E)[None])
    put("token", np.tile(np.arange(NT) * P, TOP_K)[None] + np.arange(P)[:, None] - T)
    put("spare_row", T + np.arange(P)[:, None])
    den = np.zeros((P, P), np.float32)
    for j in range(G):
        den[j * VW + HD, j * VW:(j + 1) * VW] = 1
    put("den", den)
    cb = np.zeros((P, 5 * P), np.float32)
    cb[:, 0:P] = np.eye(P)
    cb[:, P:2 * P] = np.where(np.arange(P)[None] > np.arange(P)[:, None], NEG, 0)
    cb[:, 2 * P:3 * P] = np.where(np.arange(P)[:, None] > np.arange(P)[None], NEG, 0)
    cb[:, 3 * P:4 * P] = np.arange(P)[:, None] < np.arange(P)[None]
    cb[:, 4 * P:5 * P] = 1
    inv = 1.0 / 10000.0 ** (np.arange(0, C, 2, dtype=np.float32) / np.float32(C))
    f = np.arange(S, dtype=np.float32)[None] * inv.astype(np.float32)[:, None]
    f = np.concatenate([f, f]).astype(np.float64)
    sin = np.sin(f)
    sin[C // 2:] *= -1
    rope = np.stack([np.cos(f), sin], 1).astype(np.float32)
    return c, cb, rope



def run_steps(eng, count, body, u=2):
    for k in range(u):
        body(k, k)
    with eng.Fori(1, count // u - 1) as m:
        for q in range(u):
            body(m * u + q, 2 * u + q)
    for k in range(u * (count // u - 1), count):
        body(k, k)


def attention_plan():
    chunks = [(0, c) for c in range(QC)] + [(1, c) for c in reversed(range(QC))]
    a_items, b_items, size = [], [], []
    for n, (g, c) in enumerate(chunks):
        for i in range(CT):
            n_keys = (c * CT + i + 1) * P
            for j in range(G):
                for u in range(-(-n_keys // (2 * CH))):
                    a_items.append((min(2 * CH, n_keys - 2 * CH * u), ("A", n, g, c, i, j, u)))
        size.append(sum(w for w, x in a_items if x[1] == n))
        last = (c + 1) * CT - 1
        for kt in range(last + 1):
            w = CH - max(kt - c * CT, 0) * P
            for j in range(G):
                b_items.append((w, ("B", n, g, c, kt, j)))
                if j == 1 and kt:
                    b_items.append((0, ("PV", n, g, c, kt - 1)))
                if j == 1 and kt == 0 and n:
                    b_items.append((0, ("PV", n - 1, *chunks[n - 1], (chunks[n - 1][1] + 1) * CT - 1)))
            if kt == 0 and n:
                b_items.append((0, ("OC", n - 1, *chunks[n - 1])))
    n = len(chunks) - 1
    b_items += [(0, ("PV", n, *chunks[n], (chunks[n][1] + 1) * CT - 1)), (0, ("OC", n, *chunks[n]))]

    to_rows, to_b, to_out = 2600, 5 * 1024, 1500
    lag = max(size) + to_b + to_rows
    plan, due = [], []
    done = {"a": 0, "b": 0}

    def emit(w, item, side):
        plan.append(item)
        done[side] += w
        while due and due[0][0] <= done["a"] + done["b"]:
            plan.append(due.pop(0)[1])

    def later(distance, item):
        due.append((done["a"] + done["b"] + distance, item))
        due.sort(key=lambda x: x[0])

    at = 0
    for w, item in b_items:
        while at < len(a_items) and done["a"] < done["b"] + lag:
            emit(*a_items[at], "a")
            n = a_items[at][1][1]
            at += 1
            if at == len(a_items) or a_items[at][1][1] != n:
                plan.append(("NP", n, *chunks[n]))
                later(to_rows, ("TR", n, *chunks[n]))
        emit(w, item, "b")
        if item[0] == "OC":
            later(to_out, ("OT", *item[1:]))
    plan += [x[1] for x in due]

    spread, left = [], []
    for x, item in enumerate(plan):
        if item[0] in ("TR", "OT"):
            spread += left
            left = []
        spread.append(item)
        if item[0] == "OT":
            left = [("RC", item[1], q) for q in range(N_RC)]
        elif left and item[0] == "A":
            spread.append(left.pop(0))
        if not any(y[0] == "A" for y in plan[x:]):
            spread += left
            left = []
    return chunks, spread + left


def program(nc, io):
    ctx = ExitStack()
    with ctx:
        sb = lambda name, shape, dt=fp32: ctx.enter_context(nc.sbuf_tensor(name, shape, dt))
        sem = lambda name: ctx.enter_context(nc.semaphore(name))
        dram = lambda name, shape, dt=fp32: nc.dram_tensor(name, shape, dt, kind="Internal").ap()

        qk_parts = dram("qk_parts", [2, 3, C, T], bf16)
        v_rows = dram("v_rows", [T, NH * VW])
        attn_cols = dram("attn_cols", [C, T])
        xn2_rows = dram("xn2_rows", [T + P, D])

        const = sb("const", [P, CONST_W])
        constb = sb("constb", [P, 5 * P], bf16)
        cf = lambda n: const[:, CONST[n][0]:CONST[n][1]]
        cbf = lambda n: constb[:, CB[n][0]:CB[n][1]]
        ident, identb = cf("ident"), cbf("ident")
        out_wt = sb("out_wt", [P, D])
        out_b = sb("out_b", [P, D])
        W13, W2 = DC * 2 * H, HC * D
        SH13 = DC * (2 * H + E)
        sh_at = E * (W13 + W2)
        arena = sb("arena", [P, sh_at + SH13 + W2])
        w13 = arena[:, 0:E * W13].rearrange("p (e c n) -> p e c n", e=E, c=DC)
        w2 = arena[:, E * W13:sh_at].rearrange("p (e c n) -> p e c n", e=E, c=HC)
        sh13 = arena[:, sh_at:sh_at + SH13].rearrange("p (c n) -> p c n", c=DC)
        sh2 = arena[:, sh_at + SH13:].rearrange("p (c n) -> p c n", c=HC)
        cursor = [0]

        def carve(words, dt=fp32):
            a = arena[:, cursor[0]:cursor[0] + words]
            cursor[0] += words
            assert cursor[0] <= sh_at
            return a if dt is fp32 else a.bitcast(dt)

        rope = carve(2 * S).rearrange("p (a n) -> p a n", a=2)
        x_in = [carve(CT * D).rearrange("p (t n) -> p t n", t=CT) for _ in range(2)]
        xn_t = [carve(DC * CH).rearrange("p (c n) -> p c n", c=DC) for _ in range(2)]
        gel = [carve(CH) for _ in range(3)]
        rot = [carve(CH) for _ in range(2)]
        rest, rest_k = carve(CH), carve(CH)
        parts = [carve(2 * 3 * CH // 2, bf16).rearrange("p (a b n) -> p a b n", a=2, b=3) for _ in range(2)]
        v_out = [carve(CT * NH * VW).rearrange("p (t h w) -> p t h w", t=CT, h=NH) for _ in range(2)]
        w_in = carve(3 * D).rearrange("p (a n) -> p a n", a=3)
        w_t = carve(3 * D).rearrange("p (a c n) -> p a c n", a=3, c=DC)
        cv_w, cv_t = carve(C), carve(C)
        out_w = carve(DC * C).rearrange("p (c n) -> p c n", c=DC)
        gate_w = carve(D)
        constb_in = xn_t[1].rearrange("p c n -> p (c n)")[:, 0:5 * P]
        stack = lambda: carve(G * S // 2, bf16).rearrange("p (j n) -> p j n", j=G)
        beside = cursor[0]
        stack_q, stack_k = [stack()], [stack()]
        m_raw = carve(2 * 2 * G * CT).rearrange("p (a u i j) -> p a u i j", a=2, u=2, j=G)
        m_neg, m_rest = (carve(G * CT).rearrange("p (i j) -> p i j", j=G) for _ in range(2))
        m_parts = [carve(3 * G * CT // 2, bf16) for _ in range(2)]
        m_rows = [carve(CH // 2, bf16) for _ in range(2)]

        cursor[0] = 0
        for _ in range(1, NG):
            stack_q.append(stack())
            stack_k.append(stack())
        v_sb = [carve(TB * G * VW).rearrange("p (t j w) -> p t j w", t=TB, j=G) for _ in range(NG)]
        PS = 2 * G
        probs = carve(PS * CH).rearrange("p (s n) -> p s n", s=PS)
        o_sb = [carve(CH) for _ in range(2)]
        n_sb = [carve(CH) for _ in range(2)]
        inv_den = carve(CH)
        assert cursor[0] <= beside
        b_proj = sb("b_proj", [P, 3])
        b_v = sb("b_v", [P, C])
        stats = sb("stats", [P, CT, 6])
        mv = sb("mv", [P, CT, 2])
        rstd, var, newton = (sb(n, [P, CT]) for n in ("rstd", "var", "newton"))
        N_NORM = 14

        attn_cur = sb("attn_cur", [P, 2, P])
        xg = sb("xg", [P, 2, D])
        xg_t = sb("xg_t", [P, 2, DC, P])
        silu = sb("silu", [P, H])
        act_sb = sb("act_sb", [P, 2, HP])
        act_t = sb("act_t", [P, 2, HC, P])
        y_sb = sb("y_sb", [P, 2, D])
        XR = 8
        x1 = sb("x1", [P, XR, D])
        logits = sb("logits", [P, NT, E])
        weight = sb("weight", [P, TOP_K * NT])
        slot_i = sb("slot_i", [P, TOP_K * NT], i32)
        idx_i = sb("idx_i", [P, NB], i32)
        cur_i = sb("cur_i", [P, 2], i32)
        cur_s = sb("cur_s", [P, 2], i32)
        eid_i = sb("eid_i", [1, NB], i32)
        sel_b = sb("sel_b", [P, NT * E], bf16)
        GR = 4
        x1f, oh_at = x1[:, :, :].rearrange("p a n -> p (a n)"), 6 * NT * E
        oh_row = x1f[:, oh_at:oh_at + 2 * GR * P].rearrange("p (k r n) -> p k r n", k=2, r=GR)
        oh_at += 2 * GR * P
        oh_blk = x1f[:, oh_at:oh_at + 2 * GR * 2 * NB].rearrange("p (k r a n) -> p k r a n", k=2, r=GR, a=2)
        token_rel = sb("token_rel", [P, TOP_K * NT])
        w_slot = sb("w_slot", [P, NB])
        per_e = sb("per_e", [P, 5 * E])
        per_ei = sb("per_ei", [P, E], i32)
        per_s = sb("per_s", [P, 6 * NT])
        slot_f = sb("slot_f", [P, 3, TOP_K * NT])
        slot_t = sb("slot_t", [P, TOP_K * NT], i32)
        eid_f = sb("eid_f", [1, NB])

        psum = ctx.enter_context(nc.psum_tensor("psum", [P, 8, 512], fp32))
        m_bank = psum[0:3 * G, 7, 0:CH // 2].bitcast(bf16)

        s_c = sem("constants_loaded")
        s_cb = sem("bfloat16_constants_ready")
        s_pw = sem("projection_weights_loaded")
        N_PW = 11
        s_rld = sem("rope_loaded")
        s_wt, s_wte = sem("weights_transposed"), sem("weights_t_ready")
        s_x = [sem(f"x_loaded_{i}") for i in range(2)]
        s_ln = sem("ln_chain")
        s_xn = sem("xn_ready")
        s_xt, s_xte = sem("xn_transposed"), sem("xn_t_ready")
        s_pc, s_pq, s_pk = sem("kv_projected"), sem("q_projected"), sem("k_projected")
        s_gc = sem("kv_gelu_ready")
        s_vp = sem("v_projected")
        s_half = sem("rope_halves_ready")
        s_rope = sem("rope_ready")
        s_gel = sem("qk_gelu_ready")
        s_split = sem("split_chain")
        s_parts, s_parts_k, s_split_k = sem("q_parts_ready"), sem("k_parts_ready"), sem("k_split_chain")
        s_vout = sem("v_ready")
        s_vpad = sem("v_pad_set")
        s_pst = [sem(f"parts_stored_{i}") for i in range(2)]
        s_kone = sem("k_ones_set")
        s_stack = [sem(f"stacks_loaded_{g}") for g in range(NG)]
        N_STACK = 2 * len(TERMS)
        s_vld = sem("values_loaded")
        s_a, s_ar = sem("a_scores_ready"), sem("a_scores_used")
        s_npc, s_np = sem("max_chain"), sem("max_parts_ready")
        s_b, s_e = sem("b_scores_ready"), sem("probs_ready")
        s_pv = sem("pv_groups_done")
        s_oe = sem("chunk_output_copied")
        s_m, s_me = sem("misc_bank_ready"), sem("misc_bank_used")
        s_mld = [sem(f"max_rows_loaded_{i}") for i in range(2)]
        s_att = sem("attention_chunks_ready")
        s_ast = [sem(f"attention_chunks_stored_{i}") for i in range(2)]
        s_zero_y, s_spare = sem("zero_rows_set"), sem("spare_rows_stored")
        s_w, s_sw = sem("expert_weights_loaded"), sem("shared_weights_loaded")
        s_zero = sem("act_pad_zeroed")

        def pipe(tag):
            names = ("xg_ready", "xt", "xte", "up", "silu", "a", "at", "ate", "dn", "ye", "rows_0", "rows_1",
                     "stored_0", "stored_1")
            return {x: sem(f"{tag}_{x}") for x in names}

        sh, ro = pipe("shared"), pipe("routed")
        s_xr = [sem(f"x_row_loaded_{i}") for i in range(XR)]
        s_ac = [sem(f"attention_tile_loaded_{i}") for i in range(2)]
        s_op, s_x1 = sem("out_projected"), sem("x1_ready")
        s_fl = sem("front_chain")
        s_xns = [sem(f"xn2_stored_{i}") for i in range(2)]
        s_lg, s_sig = sem("logits_ready"), sem("sigmoid_ready")
        s_r = sem("route_chain")
        s_sel, s_cnt = sem("selected_ready"), sem("counts_ready")
        s_oh, s_ohp = sem("one_hot_ready"), sem("one_hot_used")
        s_idx = sem("indices_ready")
        s_cur, s_curs = sem("gather_indices_copied"), sem("scatter_indices_copied")
        chunks, plan = attention_plan()
        NS = len(chunks)
        n_a, n_b, n_pv = (sum(x[0] == w for x in plan) for w in ("A", "B", "PV"))
        misc = [x[:2] for x in plan if x[0] in ("TR", "OT")]
        N_MISC = len(misc)
        x_chunk = io["x"].rearrange("(n t p) d -> n p t d", t=CT, p=P)
        rows = lambda a, n: a[bass.ds(n * P, P), :]
        v_tiles = v_rows.rearrange("(t p) w -> p t w", p=P)
        used = lambda n, k: 8 * (n - k % 2)
        w1_rows, w3_rows, w2_rows = (io[w].rearrange("e r n -> (e r) n") for w in ("w1", "w3", "w2"))
        used_x = lambda n, k: 16 // XR * (n - k % XR)

        def wait_apart(eng, s, value):
            value = value if isinstance(value, int) else eng.to_reg(value)
            eng.wait_ge(s_c, 32)
            eng.wait_ge(s, value)

        block = ctx.enter_context(nc.Block())

        @block.sync
        def _(sp):
            sp.dma_start(const[:, :], io["const"]).then_inc(s_c, 16)
            sp.dma_start(constb_in, io["constb"]).then_inc(s_c, 16)
            for a, n in enumerate(("wq", "wk", "wc")):
                sp.dma_start(w_in[:, a, :], io[n]).then_inc(s_pw, 16)
            sp.dma_start(cv_w, io["wv"]).then_inc(s_pw, 16)
            sp.dma_start(out_w, io["wo"].rearrange("(c p) n -> p c n", p=P)).then_inc(s_pw, 16)
            sp.dma_start(gate_w[0:E, :], io["gate"]).then_inc(s_pw, 16)
            for a, n in enumerate(("bq", "bk", "bc")):
                sp.dma_start(b_proj[:, a:a + 1], io[n].rearrange("(p a) -> p a", a=1)).then_inc(s_pw, 16)
            sp.dma_start(b_v[:, :], io["bv"].rearrange("(a n) -> a n", a=1).broadcast_to([P, C])).then_inc(s_pw, 16)
            sp.dma_start(out_b[:, :], io["bo"].rearrange("(a n) -> a n", a=1).broadcast_to([P, D])).then_inc(s_pw, 16)

            def load_x(n, k):
                if k >= 2:
                    sp.wait_ge(s_xt, n - 1)
                sp.dma_start(x_in[k % 2], x_chunk[bass.ds(n, 1)].rearrange("a p t d -> p (a t) d")).then_inc(s_x[k % 2], 16)

            def load_stacks(b, g):
                for which, stack in enumerate((stack_q[g], stack_k[g])):
                    for r, term in enumerate(TERMS):
                        src = qk_parts[which, term[which], g * G * HD:(g + 1) * G * HD, b * S:(b + 1) * S]
                        sp.dma_start(stack[r * HD:(r + 1) * HD, :, :],
                                     src.rearrange("(j d) n -> d j n", j=G)).then_inc(s_stack[g], 16)

            def load_values(b):
                for g in range(NG):
                    sp.dma_start(v_sb[g].rearrange("p t j w -> p t (j w)"),
                                 v_tiles[:, b * TB:(b + 1) * TB, g * G * VW:(g + 1) * G * VW]).then_inc(s_vld, 16)

            def projections(n, k):
                if k < NCH - 2:
                    load_x(n + 2, k + 2)
                if k == NCH - 2:
                    for i in range(2):
                        sp.wait_ge(s_pst[i], 16 * 3 * (NCH - 2) // 2)
                    load_stacks(0, 0)
                sp.wait_ge(s_vout, n + 1)
                sp.dma_start(v_tiles[:, bass.ds(n * CT, CT)],
                             v_out[k % 2].rearrange("p t h w -> p t (h w)")).then_inc(s_pst[k % 2], 16)
                sp.wait_ge(s_parts, n + 1)
                sp.wait_ge(s_parts_k, n + 1)
                for a in range(2):
                    sp.dma_start(qk_parts[a][:, :, bass.ds(n * CH, CH)].rearrange("b p n -> p b n"),
                                 parts[k % 2][:, a]).then_inc(s_pst[k % 2], 16)

            load_x(0, 0)
            sp.dma_start(rope, io["rope"]).then_inc(s_rld, 16)
            load_x(1, 1)
            sp.dma_start(sh13[:, :, 0:H], io["sw1"].rearrange("(c p) n -> p c n", p=P)).then_inc(s_sw, 16)
            sp.dma_start(sh13[:, :, H + E:], io["sw3"].rearrange("(c p) n -> p c n", p=P)).then_inc(s_sw, 16)
            sp.dma_start(sh2[:, 0:HC - 1, :], io["sw2"][0:(HC - 1) * P].rearrange("(c p) n -> p c n", p=P)).then_inc(s_sw, 16)
            sp.dma_start(sh2[0:HL, HC - 1, :], io["sw2"][(HC - 1) * P:]).then_inc(s_sw, 16)
            run_steps(sp, NCH, projections)
            for i in range(2):
                sp.wait_ge(s_pst[i], 16 * 3 * NCH // 2)

            for k in range(XR - 1):
                sp.dma_start(x1[:, k, :], rows(io["x"], k)).then_inc(s_xr[k], 16)
            for b in range(B):
                load_stacks(b, 1)
                load_values(b)
                for item in plan:
                    if item[0] == "TR":
                        _, n, g, c = item
                        sp.wait_ge(s_me, b * N_MISC + misc.index(("TR", n)) + 1)
                        sp.dma_start(stack_q[g][KR:KM, :, c * CH:(c + 1) * CH],
                                     m_rows[n % 2][0:3 * G, :]).then_inc(s_mld[n % 2], 16)
                    if item[0] == "OT":
                        _, n, g, c = item
                        sp.wait_ge(s_att, b * NS + n + 1)
                        for j in range(G):
                            h = (g * G + j) * HD
                            sp.dma_start(attn_cols[h:h + HD, b * S + c * CH:b * S + (c + 1) * CH],
                                         n_sb[n % 2][j * VW:j * VW + HD, :]).then_inc(s_ast[n % 2], 16)
                        if b < B - 1 and n == QC - 1:
                            load_stacks(b + 1, 0)
                sp.wait_ge(s_pv, (b + 1) * n_pv)
            for i in range(2):
                sp.wait_ge(s_ast[i], 16 * G * B * NS // 2)

            def load_attn(n, k):
                if k >= 2:
                    wait_apart(sp, s_op, n - 1)
                sp.dma_start(attn_cur[:, k % 2, :], attn_cols[:, bass.ds(n * P, P)]).then_inc(s_ac[k % 2], 16)

            def load_row(n, k):
                if k >= XR:
                    sp.wait_ge(sh["ye"], n - (XR - 1))
                sp.dma_start(x1[:, k % XR, :], rows(io["x"], n)).then_inc(s_xr[k % XR], 16)

            def store_xn2(n, k):
                sp.wait_ge(sh["xg_ready"], n + 1)
                sp.dma_start(rows(xn2_rows, n), xg[:, k % 2, :]).then_inc(s_xns[k % 2], 16)

            def store_y(ss, dst, n, k):
                sp.wait_ge(ss["ye"], n + 1)
                sp.dma_start(rows(dst, n), y_sb[:, k % 2, :]).then_inc(ss[f"stored_{k % 2}"], 16)

            def load_expert(n, part):
                u13 = arena[:, bass.ds(n * (W13 * E // NT), W13)].rearrange("p (c n) -> p c n", c=DC)
                u2 = arena[:, bass.ds(n * (W2 * E // NT) + E * W13, W2)].rearrange("p (c n) -> p c n", c=HC)
                d, h = D * E // NT, H * E // NT
                room, rows_of = (
                    (u13[:, :, 0:H], w1_rows[bass.ds(n * d, D), :].rearrange("(c p) n -> p c n", p=P)),
                    (u13[:, :, H:], w3_rows[bass.ds(n * d, D), :].rearrange("(c p) n -> p c n", p=P)),
                    (u2[:, 0:HC - 1, :], w2_rows[bass.ds(n * h, (HC - 1) * P), :].rearrange("(c p) n -> p c n", p=P)),
                    (u2[0:HL, HC - 1, :], w2_rows[bass.ds(n * h + (HC - 1) * P, HL), :]))[part]
                sp.dma_start(room, rows_of).then_inc(s_w, 16)

            def shared(n, k):
                if k < NT - 3:
                    load_attn(n + 3, k + 3)
                if k < NT - 2:
                    store_xn2(n + 2, k + 2)
                if k >= 1:
                    store_y(sh, io["out"], n - 1, k - 1)
                if k < NT - (XR - 1):
                    load_row(n + XR - 1, k + XR - 1)
                load_expert(n - k % 4, k % 4)

            load_attn(0, 0)
            load_attn(1, 1)
            load_attn(2, 2)
            store_xn2(0, 0)
            store_xn2(1, 1)
            run_steps(sp, NT, shared, XR)
            store_y(sh, io["out"], NT - 1, NT - 1)

        @block.gpsimd
        def _(pool):
            def split_k(n, k):
                if k >= 2:
                    wait_apart(pool, s_pst[k % 2], 3 * used(n, k))
                if k >= 1:
                    wait_apart(pool, s_parts_k, n)
                wait_apart(pool, s_gel, 2 * n + 2)
                pt = parts[k % 2]
                nc.gpsimd.tensor_copy(pt[:, 1, 0, :], gel[1]).then_inc(s_split_k, 1)
                pool.wait_ge(s_split_k, 3 * n + 1)
                nc.gpsimd.tensor_tensor(rest_k, gel[1], pt[:, 1, 0, :], ALU.subtract).then_inc(s_split_k, 1)
                wait_apart(pool, s_split_k, 3 * n + 2)
                nc.gpsimd.tensor_copy(pt[:, 1, 1, :], rest_k).then_inc(s_split_k, 1)
                pool.wait_ge(s_split_k, 3 * n + 3)
                nc.gpsimd.tensor_tensor(pt[:, 1, 2, :], rest_k, pt[:, 1, 1, :], ALU.subtract).then_inc(s_parts_k, 1)

            nc.gpsimd.memset(act_sb[:, :, H:], 0.0).then_inc(s_zero, 1)
            for i in range(2):
                nc.gpsimd.memset(v_out[i][:, :, :, HD + 1:], 0.0).then_inc(s_vpad, 1)
                nc.gpsimd.memset(v_out[i][:, :, :, HD:HD + 1], 1.0).then_inc(s_vpad, 1)
            nc.gpsimd.memset(y_sb[:, 0, :], 0.0).then_inc(s_zero_y, 1)
            pool.wait_ge(s_zero_y, 1)
            for rows_of in (xn2_rows, io["out"]):
                pool.dma_start(rows_of[T:T + P, :], y_sb[:, 0, :]).then_inc(s_spare, 16)
            nc.gpsimd.memset(stack_k[0][KR:KM], 1.0).then_inc(s_kone, 1)
            pool.wait_ge(s_kone, 1)
            run_steps(pool, NCH, split_k)
            for i in range(2):
                pool.wait_ge(s_pst[i], 16 * 3 * NCH // 2)
            for g in range(1, NG):
                nc.gpsimd.memset(stack_k[g][KR:KM], 1.0).then_inc(s_kone, 1)

            pool.wait_ge(s_idx, 1)
            pool.wait_ge(s_spare, 32)
            for i in range(2):
                pool.wait_ge(s_xns[i], 16 * NT // 2)

            def gather(n, k):
                if k >= 2:
                    pool.wait_ge(ro["xt"], n - 1)
                nc.gpsimd.tensor_copy(cur_i[:, k % 2:k % 2 + 1], idx_i[:, bass.ds(n, 1)]).then_inc(s_cur, 1)
                wait_apart(pool, s_cur, n + 1)
                nc.gpsimd.indirect_dma_start(
                    out=xg[:, k % 2, :], out_offset=None, in_=xn2_rows[:, :],
                    in_offset=bass.IndirectOffsetOnAxis(ap=cur_i[:, k % 2:k % 2 + 1], axis=0),
                ).then_inc(ro[f"rows_{k % 2}"], 16)

            def scatter(n, k):
                pool.wait_ge(ro["ye"], n + 1)
                if k >= 1:
                    pool.wait_ge(ro[f"stored_{(k - 1) % 2}"], used(n - 1, k - 1) + 16)
                nc.gpsimd.tensor_copy(cur_s[:, k % 2:k % 2 + 1], idx_i[:, bass.ds(n, 1)]).then_inc(s_curs, 1)
                wait_apart(pool, s_curs, n + 1)
                nc.gpsimd.indirect_dma_start(
                    out=io["out"][:, :], out_offset=bass.IndirectOffsetOnAxis(ap=cur_s[:, k % 2:k % 2 + 1], axis=0),
                    in_=y_sb[:, k % 2, :], in_offset=None, compute_op=ALU.add,
                ).then_inc(ro[f"stored_{k % 2}"], 16)

            def routed(n, k):
                if k < NB - 2:
                    gather(n + 2, k + 2)
                if k >= 2:
                    scatter(n - 2, k - 2)

            gather(0, 0)
            gather(1, 1)
            for i in range(2):
                pool.wait_ge(sh[f"stored_{i}"], 16 * NT // 2)
            run_steps(pool, NB, routed)
            scatter(NB - 2, NB - 2)
            scatter(NB - 1, NB - 1)
            for i in range(2):
                pool.wait_ge(ro[f"stored_{i}"], 16 * ((NB + 1 - i) // 2))

        @block.scalar
        def _(act):
            act.wait_ge(s_pw, 16 * N_PW)
            for a in range(3):
                act.wait_ge(s_wt, a + 1)
                nc.scalar.copy(w_t[:, a, :, :], psum[:, a, :].rearrange("p (c n) -> p c n", c=DC)).then_inc(s_wte, 1)
            act.wait_ge(s_wt, 4)
            nc.scalar.copy(out_wt[:, :], psum[:, 3, :]).then_inc(s_wte, 1)
            act.wait_ge(s_wt, 6)
            nc.scalar.copy(cv_t, psum[:, 4, 0:C]).then_inc(s_wte, 1)
            nc.scalar.copy(sh13[:, :, H:H + E], psum[:, 4, C:C + DC * E].rearrange("p (c n) -> p c n", c=DC)).then_inc(s_wte, 1)

            def xt_copy(n, k):
                act.wait_ge(s_xt, n + 1)
                if k >= 2:
                    act.wait_ge(s_pk, n - 1)
                for c in range(DC):
                    i = nc.scalar.copy(xn_t[k % 2][:, c, :], psum[:, c, :])
                i.then_inc(s_xte, 1)

            def projections(n, k):
                act.wait_ge(s_pc, n + 1)
                if k >= 1:
                    act.wait_ge(s_vp, n)
                nc.scalar.activation(gel[2], psum[:, 6, :], ACT.Gelu, bias=b_proj[:, 2:3]).then_inc(s_gc, 1)
                if k < NCH - 1:
                    xt_copy(n + 1, k + 1)
                for a in range(2):
                    act.wait_ge(s_rope, 2 * n + a + 1)
                    if k >= 1:
                        act.wait_ge((s_parts, s_parts_k)[a], n)
                    nc.scalar.activation(gel[a], rot[a], ACT.Gelu).then_inc(s_gel, 1)

            xt_copy(0, 0)
            run_steps(act, NCH, projections)

            with act.Fori(0, B) as b:
                at_b = at_pv = 0
                for item in plan:
                    if item[0] == "B":
                        _, n, g, c, kt, j = item
                        d = max(kt - c * CT, 0)
                        act.wait_ge(s_b, b * n_b + at_b + 1)
                        if at_b >= PS:
                            act.wait_ge(s_pv, b * n_pv + at_b // G - 1)
                        nc.scalar.activation(probs[:, at_b % PS, d * P:], psum[:, 4 + at_b % 2, 0:CH - d * P], ACT.Exp,
                                             scale=float(HD) ** -0.5).then_inc(s_e, 1)
                        at_b += 1
                    if item[0] == "PV":
                        at_pv += 1
                    if item[0] == "OC":
                        n = item[1]
                        act.wait_ge(s_pv, b * n_pv + at_pv)
                        if n >= 2:
                            act.wait_ge(s_att, b * NS + n - 1)
                        nc.scalar.copy(o_sb[n % 2], psum[:, 6, :]).then_inc(s_oe, 1)
                act.wait_ge(s_pv, (b + 1) * n_pv)
                act.wait_ge(s_att, (b + 1) * NS)

            def experts(ss, count, u):
                def xt_copy(n, k):
                    act.wait_ge(ss["xt"], n + 1)
                    if k >= 2:
                        act.wait_ge(ss["up"], n - 1)
                    nc.scalar.copy(xg_t[:, k % 2], psum[:, 0, :].rearrange("p (c n) -> p c n", c=DC)).then_inc(ss["xte"], 1)

                def at_copy(n, k):
                    act.wait_ge(ss["at"], n + 1)
                    if k >= 2:
                        act.wait_ge(ss["dn"], n - 1)
                    nc.scalar.copy(act_t[:, k % 2], psum[:, 5, 0:HP].rearrange("p (c n) -> p c n", c=HC)).then_inc(ss["ate"], 1)

                def step(n, k):
                    if k < count - 1:
                        xt_copy(n + 1, k + 1)
                    if k >= 1:
                        at_copy(n - 1, k - 1)
                    act.wait_ge(ss["up"], n + 1)
                    if k >= 1:
                        act.wait_ge(ss["a"], n)
                    nc.scalar.activation(silu[:, :], psum[:, 1 + k % 2, 0:H], ACT.Silu).then_inc(ss["silu"], 1)

                xt_copy(0, 0)
                run_steps(act, count, step, u)
                at_copy(count - 1, count - 1)

            experts(sh, NT, XR)
            act.wait_ge(s_lg, NT)
            nc.scalar.activation(logits[:, :, :], logits[:, :, :], ACT.Sigmoid).then_inc(s_sig, 1)
            experts(ro, NB, 2)

        @block.tensor
        def _(pe):
            pe.wait_ge(s_c, 32)
            pe.wait_ge(s_pw, 16 * N_PW)
            for a in range(3):
                for c in range(DC):
                    i = nc.tensor.transpose(psum[:, a, c * P:(c + 1) * P], w_in[:, a, c * P:(c + 1) * P], ident)
                i.then_inc(s_wt, 1)
            for c in range(DC):
                i = nc.tensor.transpose(psum[:, 3, c * P:(c + 1) * P], out_w[:, c, :], ident)
            i.then_inc(s_wt, 1)
            nc.tensor.transpose(psum[:, 4, 0:C], cv_w, ident).then_inc(s_wt, 1)
            for c in range(DC):
                i = nc.tensor.transpose(psum[:, 4, C + c * E:C + (c + 1) * E], gate_w[0:E, c * P:(c + 1) * P], ident[0:E, 0:E])
            i.then_inc(s_wt, 1)

            def transposes(n, k):
                pe.wait_ge(s_xn, n + 1)
                if k >= 1:
                    pe.wait_ge(s_xte, n)
                for c in range(DC):
                    for t in range(CT):
                        i = nc.tensor.transpose(psum[:, c, t * P:(t + 1) * P], x_in[k % 2][:, t, c * P:(c + 1) * P], ident)
                i.then_inc(s_xt, 1)

            def projections(n, k):
                pe.wait_ge(s_xte, n + 1)
                for which, bank, done in ((2, 6, s_pc), (0, 4, s_pq), (1, 5, s_pk)):
                    if k >= 1 and which == 2:
                        pe.wait_ge(s_gc, n)
                    elif k >= 1:
                        pe.wait_ge(s_rope, 2 * n - 1 + which)
                    for c in range(DC):
                        i = nc.tensor.matmul(psum[:, bank, :], w_t[:, which, c, :], xn_t[k % 2][:, c, :],
                                             start=c == 0, stop=c == DC - 1)
                    i.then_inc(done, 1)
                if k < NCH - 1:
                    transposes(n + 1, k + 1)
                pe.wait_ge(s_gc, n + 1)
                if k >= 1:
                    pe.wait_ge(s_vout, n)
                for t in range(CT):
                    i = nc.tensor.matmul(psum[:, 7, t * P:(t + 1) * P], gel[2][:, t * P:(t + 1) * P], cv_t, start=True, stop=True)
                i.then_inc(s_vp, 1)

            pe.wait_ge(s_wte, 6)
            transposes(0, 0)
            run_steps(pe, NCH, projections)

            pe.wait_ge(s_cb, 1)
            pe.wait_ge(s_xte, NCH)
            with pe.Fori(0, B) as b:
                at_a = at_b = at_pv = at_m = 0
                for item in plan:
                    if item[0] == "A":
                        _, n, g, c, i, j, u = item
                        if i == j == u == 0:
                            pe.wait_ge(s_stack[g], (b + 1) * (16 * N_STACK))
                        qt = c * CT + i
                        if at_a >= 2:
                            pe.wait_ge(s_ar, b * n_a + at_a - 1)
                        bank = 2 * (at_a % 2)
                        end = min(2 * CH * (u + 1), (qt + 1) * P)
                        for k0 in range(2 * CH * u, end, CH):
                            w = min(CH, end - k0)
                            diagonal = k0 + w == (qt + 1) * P
                            ins = nc.tensor.matmul(psum[:, bank, 0:w], stack_q[g][0:KR, j, qt * P:(qt + 1) * P],
                                                   stack_k[g][0:KR, j, k0:k0 + w], start=True, stop=not diagonal)
                            if diagonal:
                                ins = nc.tensor.matmul(psum[:, bank, w - P:w], identb, cbf("mask"), start=False, stop=True)
                            bank += 1
                        ins.then_inc(s_a, 1)
                        at_a += 1
                    if item[0] == "B":
                        _, n, g, c, kt, j = item
                        if at_b == 0:
                            pe.wait_ge(s_kone, NG)
                        if kt == j == 0:
                            pe.wait_ge(s_mld[n % 2], b * (16 * NS // 2) + 16 * (n // 2 + 1))
                        d = max(kt - c * CT, 0)
                        if at_b >= 2:
                            pe.wait_ge(s_e, b * n_b + at_b - 1)
                        bank = 4 + at_b % 2
                        diagonal = kt >= c * CT
                        ins = nc.tensor.matmul(psum[:, bank, 0:CH - d * P], stack_k[g][0:KM, j, kt * P:(kt + 1) * P],
                                               stack_q[g][0:KM, j, c * CH + d * P:(c + 1) * CH], start=True, stop=not diagonal)
                        if diagonal:
                            ins = nc.tensor.matmul(psum[:, bank, 0:P], identb, cbf("mask_t"), start=False, stop=True)
                        ins.then_inc(s_b, 1)
                        at_b += 1
                    if item[0] == "PV":
                        _, n, g, c, kt = item
                        last = (c + 1) * CT - 1
                        d = max(kt - c * CT, 0)
                        if kt == 0 and n >= 1:
                            pe.wait_ge(s_oe, b * NS + n)
                        if at_pv == 0:
                            pe.wait_ge(s_vld, (b + 1) * (16 * NG))
                        pe.wait_ge(s_e, b * n_b + (at_pv + 1) * G)
                        for j in range(G):
                            ins = nc.tensor.matmul(psum[VW * j:VW * (j + 1), 6, d * P:], v_sb[g][:, kt, j, :],
                                                   probs[:, (at_pv * G + j) % PS, d * P:], start=kt == 0, stop=kt == last)
                        ins.then_inc(s_pv, 1)
                        at_pv += 1
                    if item[0] in ("TR", "OT"):
                        n = item[1]
                        if at_m == 0:
                            pe.wait_ge(s_vout, NCH)
                            pe.wait_ge(s_rope, 2 * NCH)
                        if at_m >= 1:
                            pe.wait_ge(s_me, b * N_MISC + at_m)
                        at_m += 1
                    if item[0] == "TR":
                        pe.wait_ge(s_np, b * NS + n + 1)
                        for i in range(CT):
                            ins = nc.tensor.transpose(m_bank[:, i * P:(i + 1) * P], m_parts[n % 2][:, i * 3 * G:(i + 1) * 3 * G], identb)
                        ins.then_inc(s_m, 1)
                    if item[0] == "OT":
                        pe.wait_ge(s_oe, b * NS + n + 1)
                        nc.tensor.matmul(psum[:, 7, :], cf("den"), o_sb[n % 2], start=True, stop=True).then_inc(s_m, 1)
                pe.wait_ge(s_ar, (b + 1) * n_a)
                pe.wait_ge(s_e, (b + 1) * n_b)
                pe.wait_ge(s_oe, (b + 1) * NS)
                pe.wait_ge(s_me, (b + 1) * N_MISC)

            def experts(ss, count, shared, u):
                def front(n, k):
                    pe.wait_ge(s_ac[k % 2], used(n, k) + 16)
                    if k >= 1:
                        pe.wait_ge(s_x1, n)
                    nc.tensor.matmul(psum[:, 7, :], attn_cur[:, k % 2, :], out_wt[:, :], start=True, stop=True).then_inc(s_op, 1)

                def xt(n, k):
                    if shared:
                        pe.wait_ge(ss["xg_ready"], n + 1)
                    else:
                        pe.wait_ge(ss[f"rows_{k % 2}"], used(n, k) + 16)
                    if k >= 1:
                        pe.wait_ge(ss["xte"], n)
                    for c in range(DC):
                        i = nc.tensor.transpose(psum[:, 0, c * P:(c + 1) * P], xg[:, k % 2, c * P:(c + 1) * P], ident)
                    i.then_inc(ss["xt"], 1)

                def at(n, k):
                    pe.wait_ge(ss["a"], n + 1)
                    if k >= 1:
                        pe.wait_ge(ss["ate"], n)
                    for c in range(HC):
                        i = nc.tensor.transpose(psum[:, 5, c * P:(c + 1) * P], act_sb[:, k % 2, c * P:(c + 1) * P], ident)
                    i.then_inc(ss["at"], 1)

                def up(n, k, e):
                    pe.wait_ge(ss["xte"], n + 1)
                    if k >= 2:
                        pe.wait_ge(ss["a"], n - 1)
                        if shared:
                            pe.wait_ge(s_lg, n - 1)
                    for q, bank in enumerate((1, 3)):
                        for c in range(DC):
                            if shared:
                                rhs = sh13[:, c, (0, H + E)[q]:(H + E, 2 * H + E)[q]]
                            else:
                                rhs = w13[:, bass.ds(e, 1), c, q * H:(q + 1) * H].rearrange("p a n -> p (a n)")
                            w = H + E if shared and q == 0 else H
                            i = nc.tensor.matmul(psum[:, bank + k % 2, 0:w], xg_t[:, k % 2, c, :], rhs, start=c == 0, stop=c == DC - 1)
                    i.then_inc(ss["up"], 1)

                def down(n, k, e):
                    pe.wait_ge(ss["ate"], n + 1)
                    if k >= 1:
                        pe.wait_ge(ss["ye"], n)
                    for c in range(HC):
                        r = P if c < HC - 1 else HL
                        rhs = sh2[0:r, c, :] if shared else w2[0:r, bass.ds(e, 1), c, :].rearrange("p a n -> p (a n)")
                        i = nc.tensor.matmul(psum[:, 6, :], act_t[0:r, k % 2, c, :], rhs, start=c == 0, stop=c == HC - 1)
                    i.then_inc(ss["dn"], 1)

                def expert(n):
                    return None if shared else pe.value_load(eid_i[0:1, bass.ds(n, 1)], min_val=0, max_val=E - 1)

                def step(n, k):
                    if shared and k < count - 2:
                        front(n + 2, k + 2)
                    if k < count - 1:
                        xt(n + 1, k + 1)
                    if k >= 1:
                        at(n - 1, k - 1)
                    up(n, k, expert(n))
                    if k >= 1:
                        down(n - 1, k - 1, expert(n - 1))

                if shared:
                    front(0, 0)
                    front(1, 1)
                xt(0, 0)
                run_steps(pe, count, step, u)
                at(count - 1, count - 1)
                down(count - 1, count - 1, expert(count - 1))

            pe.wait_ge(s_sw, 16 * 4)
            experts(sh, NT, True, XR)
            pe.wait_ge(s_sel, 1)
            nc.tensor.matmul(psum[:, 7, 0:NT * E], cbf("before"), sel_b[:, :], start=True, stop=True)
            nc.tensor.matmul(psum[:, 7, NT * E:], cbf("ones"), sel_b[:, :], start=True, stop=True).then_inc(s_cnt, 1)

            def one_hot(n, k):
                pe.wait_ge(s_oh, n + 1)
                for r in range(GR):
                    i = nc.tensor.matmul(psum[:, 0, 0:2 * NB], oh_row[:, k % 2, r, :], oh_blk[:, k % 2, r].rearrange("p a n -> p (a n)"),
                                         start=k == 0 and r == 0, stop=k == TOP_K * NT // GR - 1 and r == GR - 1)
                i.then_inc(s_ohp, 1)

            run_steps(pe, TOP_K * NT // GR, one_hot)
            pe.wait_ge(s_idx, 1)
            pe.wait_ge(s_w, 16 * 4 * E)
            experts(ro, NB, False, 2)

        @block.vector
        def _(dve):
            def link(ins, s, value):
                ins.then_inc(s, 1)
                dve.wait_ge(s, value)

            def norm_stats(tiles, s, at):
                for t, x in enumerate(tiles):
                    i = nc.vector.bn_stats(stats[:, t, :], x)
                i.then_inc(s, 1)
                wait_apart(dve, s, at + 1)
                for t in range(len(tiles)):
                    i = nc.vector.bn_aggr(mv[:, t, :], stats[:, t, :])
                link(i, s, at + 2)
                m = len(tiles)
                v, y, t = var[:, 0:m], rstd[:, 0:m], newton[:, 0:m]
                link(nc.vector.tensor_scalar(v, mv[:, 0:m, 1], EPS, None, ALU.add), s, at + 3)
                link(nc.vector.tensor_scalar(t.bitcast(i32), v.bitcast(i32), 1, None, ALU.arith_shift_right), s, at + 4)
                link(nc.vector.tensor_scalar(y.bitcast(i32), t.bitcast(i32), -1.0, float(0x5f3759df), ALU.mult, ALU.add), s, at + 5)
                for i in range(3):
                    link(nc.vector.scalar_tensor_tensor(t, y, -0.5, y, ALU.mult, ALU.mult), s, at + 6 + 3 * i)
                    link(nc.vector.tensor_tensor(t, t, v, ALU.mult), s, at + 7 + 3 * i)
                    link(nc.vector.scalar_tensor_tensor(y, t, 1.5, y, ALU.add, ALU.mult), s, at + 8 + 3 * i)

            def norm(n, k):
                dve.wait_ge(s_x[k % 2], used(n, k) + 16)
                if k >= 1:
                    dve.wait_ge(s_xn, n)
                norm_stats([x_in[k % 2][:, t, :] for t in range(CT)], s_ln, N_NORM * n)
                for t in range(CT):
                    i = nc.vector.tensor_scalar(x_in[k % 2][:, t, :], x_in[k % 2][:, t, :], mv[:, t, 0:1], rstd[:, t:t + 1],
                                                ALU.subtract, ALU.mult)
                i.then_inc(s_xn, 1)

            def projections(n, k):
                if k < NCH - 1:
                    norm(n + 1, k + 1)
                at = bass.ds(n % QC * CH, CH)
                half = C // 2
                for a, (bank, done) in enumerate(((4, s_pq), (5, s_pk))):
                    dve.wait_ge(done, n + 1)
                    if a == 1:
                        dve.wait_ge(s_rope, 2 * n + 1)
                    elif k >= 1:
                        dve.wait_ge(s_parts, n)
                    if k >= 1:
                        dve.wait_ge(s_gel, 2 * n - 1 + a)
                    nc.vector.scalar_tensor_tensor(rot[a], psum[:, bank, :], b_proj[:, a:a + 1], rope[:, 0, at], ALU.add, ALU.mult)
                    nc.vector.scalar_tensor_tensor(rest[0:half, :], psum[half:C, bank, :], b_proj[half:C, a:a + 1],
                                                   rope[half:C, 1, at], ALU.add, ALU.mult)
                    link(nc.vector.scalar_tensor_tensor(rest[half:C, :], psum[0:half, bank, :], b_proj[0:half, a:a + 1],
                                                        rope[0:half, 1, at], ALU.add, ALU.mult), s_half, 2 * n + a + 1)
                    nc.vector.tensor_tensor(rot[a], rot[a], rest, ALU.add).then_inc(s_rope, 1)
                dve.wait_ge(s_vp, n + 1)
                if k >= 2:
                    dve.wait_ge(s_pst[k % 2], 3 * used(n, k))
                for t in range(CT):
                    i = nc.vector.tensor_tensor(v_out[k % 2][:, t, :, 0:HD],
                                                psum[:, 7, t * P:(t + 1) * P].rearrange("p (h w) -> p h w", h=NH),
                                                b_v[:, :].rearrange("p (h w) -> p h w", h=NH), ALU.add)
                i.then_inc(s_vout, 1)
                dve.wait_ge(s_gel, 2 * n + 1)
                dve.wait_ge(s_rope, 2 * n + 2)
                pt = parts[k % 2]
                link(nc.vector.tensor_copy(pt[:, 0, 0, :], gel[0]), s_split, 3 * n + 1)
                link(nc.vector.tensor_tensor(rest, gel[0], pt[:, 0, 0, :], ALU.subtract), s_split, 3 * n + 2)
                link(nc.vector.tensor_copy(pt[:, 0, 1, :], rest), s_split, 3 * n + 3)
                nc.vector.tensor_tensor(pt[:, 0, 2, :], rest, pt[:, 0, 1, :], ALU.subtract).then_inc(s_parts, 1)

            dve.wait_ge(s_c, 32)
            nc.vector.tensor_copy(constb[:, :], constb_in).then_inc(s_cb, 1)
            dve.wait_ge(s_pw, 16 * N_PW)
            dve.wait_ge(s_vpad, 4)
            norm(0, 0)
            dve.wait_ge(s_rld, 16)
            run_steps(dve, NCH, projections)
            with dve.Fori(0, B) as b:
                at_a = at_m = links = 0
                n_links = 4 * NS
                for item in plan:
                    if item[0] == "A":
                        _, n, g, c, i, j, u = item
                        w = min(2 * CH, (c * CT + i + 1) * P - 2 * CH * u)
                        dve.wait_ge(s_a, b * n_a + at_a + 1)
                        bank = 2 * (at_a % 2)
                        src = psum[:, bank:bank + 2, :].rearrange("p a n -> p (a n)")[:, 0:w]
                        nc.vector.tensor_reduce(m_raw[:, n % 2, u, i, j:j + 1], src, AX.X, ALU.max).then_inc(s_ar, 1)
                        at_a += 1
                    if item[0] == "NP":
                        _, n, g, c = item
                        dve.wait_ge(s_ar, b * n_a + at_a)
                        raw = [m_raw[:, n % 2, u] for u in range(2)]
                        mp = m_parts[n % 2].rearrange("p (i a j) -> p a i j", a=3, j=G)
                        at = b * n_links + links
                        if c >= QC // 2:
                            link(nc.vector.tensor_tensor(m_neg, raw[0], raw[1], ALU.max), s_npc, at + 1)
                        else:
                            link(nc.vector.tensor_copy(m_neg, raw[0]), s_npc, at + 1)
                        link(nc.vector.tensor_scalar(mp[:, 0], m_neg, -1.0, None, ALU.mult), s_npc, at + 2)
                        link(nc.vector.scalar_tensor_tensor(m_rest, m_neg, -1.0, mp[:, 0], ALU.mult, ALU.subtract), s_npc, at + 3)
                        link(nc.vector.tensor_copy(mp[:, 1], m_rest), s_npc, at + 4)
                        nc.vector.tensor_tensor(mp[:, 2], m_rest, mp[:, 1], ALU.subtract).then_inc(s_np, 1)
                        links += 4
                    if item[0] in ("TR", "OT"):
                        at_m += 1
                    if item[0] == "TR":
                        n = item[1]
                        dve.wait_ge(s_m, b * N_MISC + at_m)
                        if n >= 2:
                            dve.wait_ge(s_mld[n % 2], b * (16 * NS // 2) + 16 * (n // 2))
                        nc.vector.tensor_copy(m_rows[n % 2][0:3 * G, :], m_bank).then_inc(s_me, 1)
                    if item[0] == "RC":
                        _, n, q = item
                        if q == 0:
                            dve.wait_ge(s_m, b * N_MISC + at_m)
                            if n >= 1:
                                dve.wait_ge(s_att, b * NS + n)
                        part = slice(q * CH // N_RC, (q + 1) * CH // N_RC)
                        ins = nc.vector.reciprocal(inv_den[:, part], psum[:, 7, part])
                        if q == N_RC - 1:
                            link(ins, s_me, b * N_MISC + at_m)
                            if n >= 2:
                                dve.wait_ge(s_ast[n % 2], b * (16 * G * NS // 2) + 16 * G * (n // 2))
                            nc.vector.tensor_tensor(n_sb[n % 2], o_sb[n % 2], inv_den, ALU.mult).then_inc(s_att, 1)
                dve.wait_ge(s_att, (b + 1) * NS)
                for i in range(2):
                    dve.wait_ge(s_mld[i], (b + 1) * (16 * NS // 2))
                    dve.wait_ge(s_ast[i], (b + 1) * (16 * G * NS // 2))

            dve.wait_ge(s_zero, 1)
            dve.wait_ge(s_spare, 32)

            def experts(ss, count, shared, u):
                def front(n, k):
                    row = x1[:, k % XR, :]
                    dve.wait_ge(s_op, n + 1)
                    dve.wait_ge(s_xr[k % XR], used_x(n, k) + 16)
                    link(nc.vector.tensor_tensor(row, row, psum[:, 7, :], ALU.add), s_x1, n + 1)
                    link(nc.vector.tensor_tensor(row, row, out_b[:, :], ALU.add), s_fl, (N_NORM + 1) * n + 1)
                    norm_stats([row], s_fl, (N_NORM + 1) * n + 1)
                    if k >= 2:
                        dve.wait_ge(ss["xt"], n - 1)
                        dve.wait_ge(s_xns[k % 2], used(n, k))
                    nc.vector.tensor_scalar(xg[:, k % 2, :], row, mv[:, 0, 0:1], rstd[:, 0:1],
                                            ALU.subtract, ALU.mult).then_inc(ss["xg_ready"], 1)

                def gated(n, k):
                    dve.wait_ge(ss["silu"], n + 1)
                    if k >= 2:
                        dve.wait_ge(ss["at"], n - 1)
                    nc.vector.tensor_tensor(act_sb[:, k % 2, 0:H], psum[:, 3 + k % 2, 0:H], silu[:, :], ALU.mult).then_inc(ss["a"], 1)
                    if shared:
                        nc.vector.tensor_copy(logits[:, bass.ds(n, 1), :].rearrange("p a e -> p (a e)"),
                                              psum[:, 1 + k % 2, H:H + E]).then_inc(s_lg, 1)

                def y(n, k):
                    dve.wait_ge(ss["dn"], n + 1)
                    if k >= 2:
                        dve.wait_ge(ss[f"stored_{k % 2}"], used(n, k))
                    if shared:
                        i = nc.vector.tensor_tensor(y_sb[:, k % 2, :], x1[:, k % XR, :], psum[:, 6, :], ALU.add)
                    else:
                        i = nc.vector.tensor_scalar(y_sb[:, k % 2, :], psum[:, 6, :], w_slot[:, bass.ds(n, 1)], None, ALU.mult)
                    i.then_inc(ss["ye"], 1)

                def step(n, k):
                    if shared and k < count - 2:
                        front(n + 2, k + 2)
                    gated(n, k)
                    if k >= 1:
                        y(n - 1, k - 1)

                if shared:
                    front(0, 0)
                    front(1, 1)
                run_steps(dve, count, step, u)
                y(count - 1, count - 1)

            experts(sh, NT, True, XR)
            for i in range(2):
                dve.wait_ge(sh[f"stored_{i}"], 16 * NT // 2)
            r_at = [0]

            def step(ins):
                r_at[0] += 1
                link(ins, s_r, r_at[0])

            te = lambda i: x1f[:, i * NT * E:(i + 1) * NT * E].rearrange("p (t e) -> p t e", e=E)
            over_e = lambda a: a.rearrange("p (t a) -> p t a", a=1).broadcast_to([P, NT, E])
            first, second, left, work, tile_total, before = (te(i) for i in range(6))
            rev = cf("rev8").rearrange("p (t e) -> p t e", e=E)
            top = [per_s[:, i * NT:(i + 1) * NT] for i in range(2)]
            pick, total, inv = (per_s[:, i * NT:(i + 1) * NT] for i in (2, 3, 4))
            dve.wait_ge(s_sig, 1)
            for q, (chosen, scores) in enumerate(((first, logits[:, :, :]), (second, left))):
                step(nc.vector.tensor_reduce(top[q], scores, AX.X, ALU.max))
                step(nc.vector.tensor_tensor(work, scores, over_e(top[q]), ALU.is_equal))
                step(nc.vector.tensor_tensor(work, work, rev, ALU.mult))
                step(nc.vector.tensor_reduce(pick, work, AX.X, ALU.max))
                step(nc.vector.tensor_tensor(chosen, rev, over_e(pick), ALU.is_equal))
                if q == 0:
                    step(nc.vector.scalar_tensor_tensor(left, first, -2.0, logits[:, :, :], ALU.mult, ALU.add))
            nc.vector.tensor_tensor(sel_b[:, :].rearrange("p (t e) -> p t e", e=E), first, second, ALU.add).then_inc(s_sel, 1)
            step(nc.vector.tensor_tensor(total, top[0], top[1], ALU.add))
            step(nc.vector.tensor_scalar(total, total, 1e-20, None, ALU.add))
            step(nc.vector.reciprocal(inv, total))
            for q in range(TOP_K):
                step(nc.vector.tensor_tensor(weight[:, q * NT:(q + 1) * NT], top[q], inv, ALU.mult))
            step(nc.vector.tensor_scalar(weight[:, :], weight[:, :], ROUTED_SCALE, None, ALU.mult))
            dve.wait_ge(s_cnt, 1)
            step(nc.vector.tensor_copy(tile_total.rearrange("p t e -> p (t e)"), psum[:, 7, NT * E:]))
            nc.vector.memset(work, 0.0).then_inc(s_r, 1)
            r_at[0] += 1
            dve.wait_ge(s_r, r_at[0])
            for e in range(E):
                i = nc.vector.tensor_tensor_scan(before[:, :, e], tile_total[:, :, e], work[:, :, e], 0.0, ALU.add, ALU.add)
            step(i)
            count, blocks, ends, base, spare = (per_e[:, i * E:(i + 1) * E] for i in range(5))
            step(nc.vector.tensor_scalar(per_ei[:, :], before[:, NT - 1, :], float(P - 1), None, ALU.add))
            step(nc.vector.tensor_scalar(per_ei[:, :], per_ei[:, :], P.bit_length() - 1, None, ALU.arith_shift_right))
            step(nc.vector.tensor_copy(blocks, per_ei[:, :]))
            step(nc.vector.tensor_tensor_scan(ends, blocks, work[:, 0, :], 0.0, ALU.add, ALU.add))
            step(nc.vector.tensor_tensor(base, ends, blocks, ALU.subtract))
            step(nc.vector.tensor_scalar(base, base, float(P), None, ALU.mult))
            step(nc.vector.tensor_tensor(before, before, tile_total, ALU.subtract))
            step(nc.vector.tensor_tensor(before, before, psum[:, 7, 0:NT * E].rearrange("p (t e) -> p t e", e=E), ALU.add))
            step(nc.vector.tensor_tensor(before, before, base.rearrange("p (a e) -> p a e", a=1).broadcast_to([P, NT, E]), ALU.add))
            for q, chosen in enumerate((first, second)):
                step(nc.vector.tensor_tensor(work, chosen, before, ALU.mult))
                step(nc.vector.tensor_reduce(slot_f[:, 0, q * NT:(q + 1) * NT], work, AX.X, ALU.add))
            step(nc.vector.tensor_copy(slot_i[:, :], slot_f[:, 0, :]))
            step(nc.vector.tensor_scalar(slot_t[:, :], slot_i[:, :], P.bit_length() - 1, None, ALU.arith_shift_right))
            step(nc.vector.tensor_copy(slot_f[:, 2, :], slot_t[:, :]))
            step(nc.vector.scalar_tensor_tensor(slot_f[:, 1, :], slot_f[:, 2, :], -float(P), slot_f[:, 0, :], ALU.mult, ALU.add))
            step(nc.vector.tensor_tensor(token_rel[:, :], cf("token"), slot_f[:, 1, :], ALU.subtract))
            be = x1f[0:1, 0:NB * E].rearrange("p (b e) -> p b e", e=E)
            step(nc.vector.tensor_tensor(be, ends[0:1, :].rearrange("p (a e) -> p a e", a=1).broadcast_to([1, NB, E]),
                                         cf("iota_be")[0:1, :].rearrange("p (b e) -> p b e", e=E), ALU.is_le))
            step(nc.vector.tensor_reduce(eid_f[:, :], be, AX.X, ALU.add))
            step(nc.vector.tensor_scalar(eid_i[:, :], eid_f[:, :], float(E - 1), None, ALU.min))

            def one_hot(n, k):
                if k >= 2:
                    dve.wait_ge(s_ohp, n - 1)
                for r in range(GR):
                    col = bass.ds(n * GR + r, 1)
                    nc.vector.tensor_scalar(oh_row[:, k % 2, r, :], cf("iota_p"), slot_f[:, 1, col], None, ALU.is_equal)
                    for a, value in enumerate((token_rel, weight)):
                        i = nc.vector.tensor_scalar(oh_blk[:, k % 2, r, a, :], cf("iota_b"), slot_f[:, 2, col], value[:, col],
                                                    ALU.is_equal, ALU.mult)
                i.then_inc(s_oh, 1)

            run_steps(dve, TOP_K * NT // GR, one_hot)
            dve.wait_ge(s_ohp, TOP_K * NT // GR)
            nc.vector.tensor_copy(w_slot[:, :], psum[:, 0, NB:2 * NB])
            nc.vector.tensor_scalar(idx_i[:, :], psum[:, 0, 0:NB], cf("spare_row"), None, ALU.add).then_inc(s_idx, 1)
            experts(ro, NB, False, 2)


_INS = {"L0_attn_x": "x", "L0_attn_CQR_w": "wq", "L0_attn_CQR_b": "bq", "L0_attn_CKR_w": "wk", "L0_attn_CKR_b": "bk",
        "L0_attn_CKV_w": "wc", "L0_attn_CKV_b": "bc", "L0_attn_CV_w": "wv", "L0_attn_CV_b": "bv", "L0_attn_OUT_w": "wo",
        "L0_attn_OUT_b": "bo", "L0_ffn_gate_w": "gate", "L0_ffn_w1": "w1", "L0_ffn_w2": "w2", "L0_ffn_w3": "w3",
        "L0_ffn_sw1": "sw1", "L0_ffn_sw2": "sw2", "L0_ffn_sw3": "sw3"}


def kernel(**inputs):
    import concourse.bacc as bacc
    from concourse.bass_utils import run_bass_kernel_spmd

    nc = bacc.Bacc("TRN2", target_bir_lowering=False, num_devices=1)
    arrays = {short: np.ascontiguousarray(inputs[name]) for name, short in _INS.items()}
    arrays["x"] = arrays["x"].reshape(T, D)
    arrays["const"], arrays["constb"], arrays["rope"] = constants()
    io = {n: nc.dram_tensor(f"in_{n}", a.shape, mybir.dt.from_np(a.dtype), kind="ExternalInput").ap() for n, a in arrays.items()}
    io["out"] = nc.dram_tensor("out_rows", [T + P, D], fp32, kind="ExternalOutput").ap()
    program(nc, io)
    r = run_bass_kernel_spmd(nc, [{f"in_{n}": a for n, a in arrays.items()}], core_ids=[0])
    return r.results[0]["out_rows"][0:T].reshape(B, S, D)
```
